# Optimizing a Trainium2 kernel written in Bass

```python
import numpy as np
import jax
import jax.numpy as jnp

def _softmax(x, axis=-1):
    return jax.nn.softmax(x, axis=axis)

def _gelu(x):
    return jax.nn.gelu(x, approximate=True)

def _silu(x):
    return jax.nn.silu(x)

def _sigmoid(x):
    return jax.nn.sigmoid(x)

def _layernorm(x, axis=-1, eps=1e-05):
    m = jnp.mean(x, axis=axis, keepdims=True)
    v = jnp.var(x, axis=axis, keepdims=True)
    return (x - m) / jnp.sqrt(v + eps)

def _scatter_add(tgt, idx, src, axis=0):
    return tgt.at[idx].add(src)

def _segment_sum(src, seg, n):
    return jax.ops.segment_sum(src, seg, n)
kernel_name = 'mk_adj_resnorm_d1_adj_r2_a88544'

def setup_inputs(seed: int=0):
    np.random.seed(seed)
    _w = jnp.asarray

    def _rec_inputs():
        import jax
        import jax.numpy as jnp
        _gk = jax.random.key(seed)
        x = 0.0002141 + 1 * jax.random.normal(jax.random.fold_in(_gk, 1), (8192, 64), jnp.float32)
        _w = (1.0 + jnp.arange(8192, dtype=jnp.float32)) ** (-0.5)
        _w = _w / _w.mean()
        _pij = jnp.clip(0.000488281 * _w[:, None] * _w[None, :], 0.0, 1.0)
        _a = jax.random.uniform(jax.random.fold_in(_gk, 2), (8192, 8192)) < _pij
        _a = jnp.logical_or(_a, jnp.eye(8192, dtype=bool))
        _af = _a.astype(jnp.float32)
        _af = _af * jax.random.uniform(jax.random.fold_in(_gk, 3), (8192, 8192), jnp.float32, 0.05, 1)
        adj = _af
        return (x, adj)
    x, adj = _rec_inputs()

    def _L0_gnn_setup():
        import jax, jax.numpy as jnp
        import numpy as np
        N, D = (6144, 64)

        def _ggc(x, adj, W, wih, whh, bih, bhh):
            m = adj @ (x @ W)
            gi = m @ wih.T + bih
            gh = x @ whh.T + bhh
            i_r, i_z, i_n = jnp.split(gi, 3, axis=-1)
            h_r, h_z, h_n = jnp.split(gh, 3, axis=-1)
            r = jax.nn.sigmoid(i_r + h_r)
            z = jax.nn.sigmoid(i_z + h_z)
            n = jnp.tanh(i_n + r * h_n)
            return (1.0 - z) * n + z * x
        key = jax.random.key(seed)
        ks = jax.random.split(key, 8)
        s = 1.0 / np.sqrt(D)
        return {'x': jax.random.normal(ks[0], (N, D), jnp.float32), 'adj': jax.random.uniform(ks[1], (N, N), jnp.float32), 'W1': jax.random.normal(ks[2], (D, D), jnp.float32) * s, 'wih1': jax.random.normal(ks[3], (3 * D, D), jnp.float32) * s, 'whh1': jax.random.normal(ks[4], (3 * D, D), jnp.float32) * s, 'bih1': jnp.zeros((3 * D,), jnp.float32), 'bhh1': jnp.zeros((3 * D,), jnp.float32), 'W2': jax.random.normal(ks[5], (D, D), jnp.float32) * s, 'wih2': jax.random.normal(ks[6], (3 * D, D), jnp.float32) * s, 'whh2': jax.random.normal(ks[7], (3 * D, D), jnp.float32) * s, 'bih2': jnp.zeros((3 * D,), jnp.float32), 'bhh2': jnp.zeros((3 * D,), jnp.float32)}
    _L0_gnn_all = _L0_gnn_setup()
    _L0_gnn_in = {k: v for k, v in _L0_gnn_all.items() if k in ('W1', 'wih1', 'whh1', 'bih1', 'bhh1', 'W2', 'wih2', 'whh2', 'bih2', 'bhh2')}
    del _L0_gnn_all
    return {'x': x, 'adj': adj, 'L0_gnn_W1': _L0_gnn_in['W1'], 'L0_gnn_wih1': _L0_gnn_in['wih1'], 'L0_gnn_whh1': _L0_gnn_in['whh1'], 'L0_gnn_bih1': _L0_gnn_in['bih1'], 'L0_gnn_bhh1': _L0_gnn_in['bhh1'], 'L0_gnn_W2': _L0_gnn_in['W2'], 'L0_gnn_wih2': _L0_gnn_in['wih2'], 'L0_gnn_whh2': _L0_gnn_in['whh2'], 'L0_gnn_bih2': _L0_gnn_in['bih2'], 'L0_gnn_bhh2': _L0_gnn_in['bhh2']}

def reference(x, adj, L0_gnn_W1, L0_gnn_wih1, L0_gnn_whh1, L0_gnn_bih1, L0_gnn_bhh1, L0_gnn_W2, L0_gnn_wih2, L0_gnn_whh2, L0_gnn_bih2, L0_gnn_bhh2):
    import jax
    import jax.numpy as jnp

    def _L0_gnn_ref(x, adj, W1, wih1, whh1, bih1, bhh1, W2, wih2, whh2, bih2, bhh2):
        import jax, jax.numpy as jnp
        import numpy as np
        N, D = (6144, 64)

        def _ggc(x, adj, W, wih, whh, bih, bhh):
            m = adj @ (x @ W)
            gi = m @ wih.T + bih
            gh = x @ whh.T + bhh
            i_r, i_z, i_n = jnp.split(gi, 3, axis=-1)
            h_r, h_z, h_n = jnp.split(gh, 3, axis=-1)
            r = jax.nn.sigmoid(i_r + h_r)
            z = jax.nn.sigmoid(i_z + h_z)
            n = jnp.tanh(i_n + r * h_n)
            return (1.0 - z) * n + z * x
        h = jax.nn.relu(_ggc(x, adj, W1, wih1, whh1, bih1, bhh1))
        return jax.nn.relu(_ggc(h, adj, W2, wih2, whh2, bih2, bhh2))
    x = _layernorm(x + _L0_gnn_ref(x, adj, L0_gnn_W1, L0_gnn_wih1, L0_gnn_whh1, L0_gnn_bih1, L0_gnn_bhh1, L0_gnn_W2, L0_gnn_wih2, L0_gnn_whh2, L0_gnn_bih2, L0_gnn_bhh2), axis=-1)
    return x

_drawn_inputs = setup_inputs


def setup_inputs(seed=0):
    import zlib

    import numpy as np

    out = dict(_drawn_inputs(seed))
    spreads = {'L0_gnn_bih1': (0.0, 0.403),
     'L0_gnn_bhh1': (0.0, 0.64),
     'L0_gnn_bih2': (0.0, 0.282),
     'L0_gnn_bhh2': (0.0, 0.431)}
    factors = {}
    for name, (base, spread) in spreads.items():
        noise = np.random.default_rng([zlib.crc32(name.encode()), seed]).standard_normal(out[name].shape)
        drawn = base * np.exp(spread * noise) if base else spread * noise
        out[name] = jnp.asarray(drawn.astype(out[name].dtype))
    for name, factor in factors.items():
        out[name] = (out[name] * factor).astype(out[name].dtype)
    return out
```

```python
import concourse.bass as bass
from concourse import mybir
from contextlib import ExitStack

F32 = mybir.dt.float32
F32R = mybir.dt.float32r
ACT = mybir.ActivationFunctionType
ALU = mybir.AluOpType
AX = mybir.AxisListType

N = 8192
D = 64
P = 128
CH = 1024
NB = N // CH
HALF = 512
KT = CH // P
NQ = 4
TQ = KT // NQ
EPS = 1e-5


class Row:

    def __init__(self, index, first_block, first_open, first_shared):
        self.index = index
        self.layer = index // NB
        self.q = index % NB
        self.n_open = NB - self.q
        self.n_shared = self.q if self.layer == 0 else 0
        self.n = self.n_open + self.n_shared
        self.block0 = first_block
        self.open0 = first_open
        self.shared0 = first_shared
        self.peeled = min(3, self.n)
        self.open_loop = (min(self.peeled, self.n_open), self.n_open)
        self.shared_loop = (max(self.peeled, self.n_open), self.n)

    def is_open(self, n):
        return n < self.n_open

    def chunk(self, n, opened):
        return n + self.q if opened else n - self.n_open


def all_rows():
    rows, b, o, s = [], 0, 0, 0
    for index in range(2 * NB):
        row = Row(index, b, o, s)
        rows.append(row)
        b, o, s = b + row.n, o + row.n_open, s + row.n_shared
    return rows


def gated_graph_layers(nc, adj_t, x_t, x, w, wih_t, whh_t, bih, bhh, out):
    rows = all_rows()
    n_blocks = rows[-1].block0 + rows[-1].n
    with ExitStack() as ctx:
        def sb(name, shape, dt=F32):
            return ctx.enter_context(nc.sbuf_tensor(name, shape, dt))

        def bank(name):
            return ctx.enter_context(nc.psum_tensor(name, [P, HALF], F32))

        def sem(name):
            return ctx.enter_context(nc.semaphore(name))

        adj_in = sb("adj_in", [P, 2 * NQ, TQ * CH])
        adj_hi = sb("adj_hi", [P, 2, TQ * CH], F32R)
        adj_lo = sb("adj_lo", [P, 2, TQ * CH], F32R)
        yz = sb("yz", [P, NB, KT, 2 * D])
        split_w = sb("split_w", [P, KT, 2 * D], F32R)
        plain_w = sb("plain_w", [P, KT, 2 * D])
        state = sb("state", [P, N])
        gate_in = sb("gate_in", [P, 2, HALF])
        rz = sb("rz", [P, 2, HALF])
        work = sb("work", [P, 2, HALF])
        fresh = sb("fresh", [P, 2, HALF])
        x_row = sb("x_row", [P, 2, KT * D])
        summed = sb("summed", [P, KT, D])
        squared = sb("squared", [P, KT, D])
        stats = sb("stats", [P, 4, KT])
        minus_half = sb("minus_half", [P, KT])
        w_in = sb("w_in", [D, 2, D])
        w_rz = sb("w_rz", [P, 2, P])
        w_n = sb("w_n", [P, 2, P])
        bias = sb("bias", [P, 2, 4])
        ident = sb("ident", [D, D])

        open_acc = [bank("open_acc0"), bank("open_acc1")]
        shared_acc = [bank("shared_acc0"), bank("shared_acc1")]
        rz_acc = [bank("rz_acc0"), bank("rz_acc1")]
        n_acc = [bank("n_acc0"), bank("n_acc1")]
        small_acc = rz_acc[0]

        x_loaded = sem("x_loaded")
        w_loaded = sem("w_loaded")
        adj_loaded = [sem(f"adj_loaded{k}") for k in range(NQ)]
        adj_used = sem("adj_used")
        hi_ready = sem("hi_ready")
        lo_ready = sem("lo_ready")
        split_hi = sem("split_hi")
        split_ready = sem("split_ready")
        plain_ready = sem("plain_ready")
        y_product = sem("y_product")
        y_ready = sem("y_ready")
        z_product = sem("z_product")
        z_ready = sem("z_ready")
        consts = sem("consts")
        ident_zero = sem("ident_zero")
        low_part = sem("low_part")
        partial_saved = sem("partial_saved")
        m_ready = sem("m_ready")
        v_ready = sem("v_ready")
        gates_ready = sem("gates_ready")
        rz_ready = sem("rz_ready")
        pre_ready = sem("pre_ready")
        n_ready = sem("n_ready")
        new_ready = sem("new_ready")
        h_ready = sem("h_ready")
        h_turned = sem("h_turned")
        h_taken = sem("h_taken")
        x_row_loaded = [sem("x_row_loaded0"), sem("x_row_loaded1")]
        var_ready = sem("var_ready")
        scale_ready = sem("scale_ready")
        norm_ready = sem("norm_ready")
        stored = sem("stored")
        dve_step = sem("dve_step")
        pool_step = sem("pool_step")

        block = ctx.enter_context(nc.Block())

        def ring(b, k):
            return (b % 2) * NQ + k

        def in_slot(b, k):
            return adj_in[:, ring(b, k), :] if isinstance(b, int) else adj_in[:, bass.ds(ring(b, k), 1), :]

        def chunk_w(c, tiles, cols):
            if isinstance(c, int):
                return yz[:, c, tiles, cols]
            return yz[:, bass.ds(c, 1), tiles, cols]

        def nodes(row, half):
            at = row.q * CH + half * HALF
            return slice(at, at + HALF)

        def h_count(row, h):
            if row.layer == 0:
                return 4 * row.q + 2 * (h + 1)
            return 4 * NB + 2 * row.q + h + 1

        @block.sync
        def _(sp):
            for part in (0, D):
                sp.dma_start(state[part:part + D, :], x_t).then_inc(x_loaded, 16)

            loads_register = sp.alloc_register("loads")

            def load(row, b, c):
                loads = 16 * b
                used = [NQ * (b - 2) + k + 1 for k in range(NQ)]
                if not isinstance(b, int):
                    sp.reg_mov(loads_register, loads)
                    loads = sp.snap(loads_register)
                for k in range(NQ):
                    if not isinstance(b, int) or b >= 2:
                        sp.wait_ge(adj_used, used[k])
                    if not isinstance(b, int) or b >= 1:
                        sp.wait_ge(adj_loaded[k], loads)
                    src = adj_t[row.q, c, k, :, :] if isinstance(c, int) else adj_t[row.q, bass.ds(c, 1), k, :, :]
                    sp.dma_start(in_slot(b, k), src).then_inc(adj_loaded[k], 16)

            for row in rows:
                for n in range(row.peeled):
                    load(row, row.block0 + n, row.chunk(n, row.is_open(n)))
                for opened, (lo, hi) in ((True, row.open_loop), (False, row.shared_loop)):
                    if hi > lo:
                        with sp.Fori(lo, hi) as n:
                            load(row, row.block0 + n, row.chunk(n, opened))

        @block.scalar
        def _(act):
            for l in range(2):
                act.dma_start(w_in[:, l, :], w[l]).then_inc(w_loaded, 16)
                act.dma_start(w_rz[0:D, l, :], wih_t[l][:, 0:P]).then_inc(w_loaded, 16)
                act.dma_start(w_rz[D:P, l, :], whh_t[l][:, 0:P]).then_inc(w_loaded, 16)
                for col, vec in ((0, bih), (1, bhh)):
                    act.dma_start(bias[:, l, col:col + 1], vec[l][0:P].rearrange("(p a) -> p a", a=1)).then_inc(w_loaded, 16)
                act.dma_start(bias[0:D, l, 2:3], bhh[l][P:3 * D].rearrange("(p a) -> p a", a=1)).then_inc(w_loaded, 16)
                act.dma_start(bias[D:P, l, 2:3], bih[l][P:3 * D].rearrange("(p a) -> p a", a=1)).then_inc(w_loaded, 16)
                act.wait_ge(consts, 1)
                act.dma_start(w_n[0:D, l, D:P], wih_t[l][:, P:3 * D]).then_inc(w_loaded, 16)
                act.dma_start(w_n[D:P, l, 0:D], whh_t[l][:, P:3 * D]).then_inc(w_loaded, 16)

            for c in range(NB):
                act.wait_ge(y_product, c + 1)
                act.activation(yz[:, c, :, 0:D], rz_acc[c % 2][:, :].rearrange("p (t d) -> p t d", d=D),
                               ACT.Copy).then_inc(y_ready, 1)

            def stage_hi(row, b, o, c, g):
                if not isinstance(b, int) or b >= 1:
                    act.wait_ge(adj_used, NQ * b + 2 * g - 2)
                if row.layer == 0:
                    act.wait_ge(y_ready, c + 1)
                else:
                    act.wait_ge(z_ready, c + 1)
                tiles = slice(4 * g, 4 * g + 4)
                act.activation(split_w[:, tiles, 0:D], chunk_w(c, tiles, slice(row.layer * D, row.layer * D + D)),
                               ACT.Copy).then_inc(split_hi, 1)

            def quarter_hi(b, k):
                act.wait_ge(adj_loaded[k], 16 * (b + 1))
                if not isinstance(b, int) or NQ * b + k >= 2:
                    act.wait_ge(adj_used, NQ * b + k - 1)
                act.activation(adj_hi[:, k % 2, :], in_slot(b, k), ACT.Copy).then_inc(hi_ready, 1)

            def evacuate(row):
                act.wait_ge(adj_used, NQ * (row.block0 + row.n))
                for h in range(2):
                    act.activation(work[0:D, h, :], open_acc[h][D:P, :], ACT.Copy).then_inc(low_part, 1)
                    if row.n_shared:
                        act.activation(state[0:D, nodes(row, h)], shared_acc[h][D:P, :], ACT.Copy).then_inc(partial_saved, 1)

            def sigmoids(row):
                for h in range(2):
                    act.wait_ge(gates_ready, 2 * row.index + h + 1)
                    act.activation(rz[:, h, :], rz_acc[h][:, :], ACT.Sigmoid, bias=bias[:, row.layer, 3:4]).then_inc(rz_ready, 1)

            def tanhs(row):
                for h in range(2):
                    act.wait_ge(pre_ready, 2 * row.index + h + 1)
                    act.activation(fresh[D:P, h, :], work[D:P, h, :], ACT.Tanh, bias=bias[D:P, row.layer, 2:3]).then_inc(n_ready, 1)

            def relus(row):
                for h in range(2):
                    act.wait_ge(new_ready, 2 * row.index + h + 1)
                    if row.layer == 0:
                        act.activation(state[D:P, nodes(row, h)], gate_in[D:P, h, :], ACT.Relu).then_inc(h_ready, 1)
                    elif row.q:
                        act.wait_ge(h_turned, row.q)
                    act.activation(fresh[0:D, h, :], gate_in[D:P, h, :], ACT.Relu).then_inc(h_ready, 1)

            def keep_z(row):
                act.wait_ge(z_product, row.q + 1)
                act.activation(yz[:, row.q, :, D:P], small_acc[:, :].rearrange("p (t d) -> p t d", d=D),
                               ACT.Copy).then_inc(z_ready, 1)

            def open_block(row, b, o, c, n=-1):
                for k in range(NQ):
                    if k % 2 == 0:
                        stage_hi(row, b, o, c, k // 2)
                    quarter_hi(b, k)
                    between(row, n, k)

            def between(row, n, k):
                if row.index == 0:
                    return
                last = rows[row.index - 1]
                if (n, k) == (0, 0):
                    evacuate(last)
                if (n, k) == (1, 0):
                    sigmoids(last)
                if (n, k) == (1, 1):
                    tanhs(last)
                if (n, k) == (1, 3):
                    relus(last)
                if (n, k) == (2, 3) and last.layer == 0:
                    keep_z(last)

            for row in rows:
                for n in range(row.peeled):
                    if row.is_open(n):
                        open_block(row, row.block0 + n, row.open0 + n, row.chunk(n, True), n)
                    else:
                        for k in range(NQ):
                            between(row, n, k)
                lo, hi = row.open_loop
                if hi > lo:
                    with act.Fori(lo, hi) as n:
                        open_block(row, row.block0 + n, row.open0 + n, row.chunk(n, True))
            for row in rows[-2:]:
                if row is rows[-1]:
                    evacuate(row)
                sigmoids(row)
                tanhs(row)
                relus(row)

        @block.vector
        def _(dve):
            steps = [0]

            def then_next(ins):
                steps[0] += 1
                ins.then_inc(dve_step, 1)
                dve.wait_ge(dve_step, steps[0])

            dve.memset(w_n[:, :, :], 0.0).then_inc(consts, 1)
            dve.wait_ge(w_loaded, 16 * 18)
            for l in range(2):
                dve.tensor_tensor(bias[:, l, 3:4], bias[:, l, 0:1], bias[:, l, 1:2], ALU.add).then_inc(consts, 1)

            def stage_lo(row, o, c, g):
                dve.wait_ge(split_hi, 2 * o + g + 1)
                tiles = slice(4 * g, 4 * g + 4)
                dve.tensor_tensor(split_w[:, tiles, D:P], chunk_w(c, tiles, slice(row.layer * D, row.layer * D + D)),
                                  split_w[:, tiles, 0:D].bitcast(F32), ALU.subtract).then_inc(split_ready, 1)

            def quarter_lo(b, o, k):
                dve.wait_ge(hi_ready, NQ * o + k + 1)
                dve.tensor_tensor(adj_lo[:, k % 2, :], in_slot(b, k), adj_hi[:, k % 2, :].bitcast(F32),
                                  ALU.subtract).then_inc(lo_ready, 1)

            def sum_m(row):
                for h in range(2):
                    m = gate_in[0:D, h, :]
                    dve.wait_ge(low_part, 2 * row.index + h + 1)
                    total = dve.tensor_tensor(m, open_acc[h][0:D, :], work[0:D, h, :], ALU.add)
                    if row.q:
                        then_next(total)
                        rest = shared_acc[h][0:D, :] if row.layer == 0 else state[0:D, nodes(row, h)]
                        total = dve.tensor_tensor(m, rest, m, ALU.add)
                    total.then_inc(m_ready, 1)

            def pre_tanh(row):
                for h in range(2):
                    dve.wait_ge(rz_ready, 2 * row.index + h + 1)
                    then_next(dve.scalar_tensor_tensor(out=work[D:P, h, :], in0=n_acc[h][0:D, :],
                                                       scalar=bias[0:D, row.layer, 2:3], in1=rz[0:D, h, :],
                                                       op0=ALU.add, op1=ALU.mult))
                    dve.tensor_tensor(work[D:P, h, :], n_acc[h][D:P, :], work[D:P, h, :], ALU.add).then_inc(pre_ready, 1)

            def norm(row):
                dve.wait_ge(h_turned, row.q + 1)
                dve.wait_ge(x_row_loaded[row.q % 2], 16 * (row.q // 2 + 1))
                if row.q:
                    dve.wait_ge(stored, 16 * row.q)
                add = dve.tensor_tensor(summed[:, :, :], small_acc[:, :].rearrange("p (t d) -> p t d", d=D),
                                        x_row[:, row.q % 2, :].rearrange("p (t d) -> p t d", d=D), ALU.add)
                add.then_inc(h_taken, 1)
                dve.wait_ge(h_taken, row.q + 1)
                then_next(dve.tensor_reduce(stats[:, 0, :], summed[:, :, :], AX.X, ALU.add))
                then_next(dve.tensor_scalar(stats[:, 1, :], stats[:, 0, :], 1.0 / D, None, ALU.mult))
                mean = stats[:, 1, :].rearrange("p (t a) -> p t a", a=1).to_broadcast([P, KT, D])
                then_next(dve.tensor_tensor(summed[:, :, :], summed[:, :, :], mean, ALU.subtract))
                then_next(dve.tensor_tensor(squared[:, :, :], summed[:, :, :], summed[:, :, :], ALU.mult))
                then_next(dve.tensor_reduce(stats[:, 2, :], squared[:, :, :], AX.X, ALU.add))
                dve.tensor_scalar(stats[:, 3, :], stats[:, 2, :], 1.0 / D, EPS, ALU.mult, ALU.add).then_inc(var_ready, 1)
                dve.wait_ge(scale_ready, row.q + 1)
                scale = stats[:, 0, :].rearrange("p (t a) -> p t a", a=1).to_broadcast([P, KT, D])
                dve.tensor_tensor(summed[:, :, :], summed[:, :, :], scale, ALU.mult).then_inc(norm_ready, 1)

            def open_block(row, b, o, c, n=-1):
                for k in range(NQ):
                    if k % 2 == 0:
                        stage_lo(row, o, c, k // 2)
                    quarter_lo(b, o, k)
                    between(row, n, k)

            def between(row, n, k):
                if row.index == 0:
                    return
                last = rows[row.index - 1]
                if (n, k) == (0, 0):
                    sum_m(last)
                if (n, k) == (1, 0):
                    pre_tanh(last)
                if (n, k) == (min(2, row.n - 1), 3) and last.layer == 1 and row.n > 1:
                    norm(last)

            for row in rows:
                for n in range(row.peeled):
                    if row.is_open(n):
                        open_block(row, row.block0 + n, row.open0 + n, row.chunk(n, True), n)
                    else:
                        for k in range(NQ):
                            between(row, n, k)
                lo, hi = row.open_loop
                if hi > lo:
                    with dve.Fori(lo, hi) as n:
                        open_block(row, row.block0 + n, row.open0 + n, row.chunk(n, True))
            for row in rows[-2:]:
                if row is rows[-1]:
                    sum_m(row)
                pre_tanh(row)
                norm(row)

        @block.gpsimd
        def _(pool):
            steps = [0]

            def then_next(ins):
                steps[0] += 1
                ins.then_inc(pool_step, 1)
                pool.wait_ge(pool_step, steps[0])

            pool.memset(ident[:, :], 0.0).then_inc(ident_zero, 1)
            pool.wait_ge(ident_zero, 1)
            pool.affine_select(out=ident[:, :], in_=ident[:, :], compare_op=ALU.not_equal, fill=1.0, base=0,
                               pattern=[[-1, D]], channel_multiplier=1).then_inc(ident_zero, 1)
            pool.memset(minus_half[:, :], -0.5).then_inc(ident_zero, 1)
            pool.wait_ge(ident_zero, 3)
            pool.wait_ge(x_loaded, 32)

            def stage_plain(b, s, c):
                for g in range(2):
                    pool.wait_ge(adj_used, NQ * b + 2 * g - 2)
                    pool.wait_ge(z_ready, c + 1)
                    tiles = slice(4 * g, 4 * g + 4)
                    pool.tensor_copy(plain_w[:, tiles, :], chunk_w(c, tiles, slice(0, P))).then_inc(plain_ready, 1)

            def after_stages(row, n):
                count = 2 * (row.shared0 + max(0, min(n, row.n) - row.n_open))
                if count:
                    pool.wait_ge(plain_ready, count)

            def copy_v(row):
                after_stages(rows[min(row.index + 1, len(rows) - 1)], 1)
                if row.index > NB:
                    pool.wait_ge(scale_ready, row.q)
                for h in range(2):
                    if row.index:
                        pool.wait_ge(h_ready, h_count(rows[row.index - 1], 1))
                    if row.layer:
                        pool.wait_ge(h_ready, h_count(rows[row.q], 1))
                    pool.tensor_copy(gate_in[D:P, h, :], state[D:P, nodes(row, h)]).then_inc(v_ready, 1)

            def mix(row):
                after_stages(rows[min(row.index + 1, len(rows) - 1)], 2)
                for h in range(2):
                    v = gate_in[D:P, h, :]
                    pool.wait_ge(n_ready, 2 * row.index + h + 1)
                    then_next(pool.tensor_tensor(v, v, fresh[D:P, h, :], ALU.subtract))
                    then_next(pool.tensor_tensor(v, v, rz[D:P, h, :], ALU.mult))
                    pool.tensor_tensor(v, v, fresh[D:P, h, :], ALU.add).then_inc(new_ready, 1)

            def load_x(row):
                if row.q >= 2:
                    pool.wait_ge(h_taken, row.q - 1)
                pool.dma_start(x_row[:, row.q % 2, :], x[row.q]).then_inc(x_row_loaded[row.q % 2], 16)

            def store(row):
                pool.wait_ge(var_ready, row.q + 1)
                pool.tensor_tensor(stats[:, 0, :], stats[:, 3, :], minus_half[:, :], ALU.pow).then_inc(scale_ready, 1)
                pool.wait_ge(norm_ready, row.q + 1)
                pool.dma_start(out[row.q], summed[:, :, :].rearrange("p t d -> p (t d)")).then_inc(stored, 16)

            for row in rows:
                for n in range(row.peeled):
                    if not row.is_open(n):
                        if n == 1:
                            pool.wait_ge(v_ready, 2 * row.index)
                        if n == 2:
                            pool.wait_ge(new_ready, 2 * row.index)
                        stage_plain(row.block0 + n, row.shared0 + n - row.n_open, row.chunk(n, False))
                    if n == 0 and row.index:
                        copy_v(rows[row.index - 1])
                    if n == 1 and row.index:
                        mix(rows[row.index - 1])
                        if row.layer:
                            load_x(rows[row.index])
                        if rows[row.index - 1].layer:
                            store(rows[row.index - 1])
                lo, hi = row.shared_loop
                if hi > lo:
                    pool.wait_ge(new_ready, 2 * row.index)
                    with pool.Fori(lo, hi) as n:
                        stage_plain(row.block0 + n, row.shared0 + n - row.n_open, row.chunk(n, False))
            mix(rows[-2])
            load_x(rows[-1])
            store(rows[-2])
            copy_v(rows[-1])
            mix(rows[-1])
            store(rows[-1])
            pool.wait_ge(stored, 16 * NB)

        @block.tensor
        def _(pe):
            pe.wait_ge(w_loaded, 16 * 18)
            pe.wait_ge(consts, 3)
            pe.wait_ge(ident_zero, 3)
            pe.wait_ge(x_loaded, 32)

            def times_w(acc, source, l):
                for t in range(KT):
                    last = pe.matmul(acc[:, t * D:(t + 1) * D], source(t), w_in[:, l, :], start=True, stop=True)
                return last

            for c in range(NB):
                if c >= 2:
                    pe.wait_ge(y_ready, c - 1)
                times_w(rz_acc[c % 2], lambda t: state[0:D, c * CH + t * P:c * CH + (t + 1) * P], 0).then_inc(y_product, 1)

            def free_acc(row, n):
                if n == 0 and row.index:
                    pe.wait_ge(m_ready, 2 * row.index)
                if n == row.n_open and row.q > 1:
                    pe.wait_ge(partial_saved, 2 * (row.q - 1))

            def open_block(row, b, o, n=-1):
                free_acc(row, n)
                for k in range(NQ):
                    if k % 2 == 0:
                        pe.wait_ge(split_ready, 2 * o + k // 2 + 1)
                    pe.wait_ge(lo_ready, NQ * o + k + 1)
                    for t in range(TQ):
                        for part in (adj_hi, adj_lo):
                            for h in range(2):
                                at = t * CH + h * HALF
                                last = pe.matmul(open_acc[h][:, :], split_w[:, TQ * k + t, :],
                                                 part[:, k % 2, at:at + HALF],
                                                 start=(n == 0 and k == 0 and t == 0 and part is adj_hi),
                                                 stop=(n == row.n_open - 1 and k == NQ - 1 and t == TQ - 1
                                                       and part is adj_lo))
                    last.then_inc(adj_used, 1)

            def shared_block(row, b, s, n=-1):
                free_acc(row, n)
                for k in range(NQ):
                    if k % 2 == 0:
                        pe.wait_ge(plain_ready, 2 * s + k // 2 + 1)
                    pe.wait_ge(adj_loaded[k], 16 * (b + 1))
                    slot = in_slot(b, k)
                    for t in range(TQ):
                        for h in range(2):
                            at = t * CH + h * HALF
                            moving = slot[:, at:at + HALF] if isinstance(b, int) else \
                                adj_in[:, bass.ds(ring(b, k), 1), at:at + HALF]
                            last = pe.matmul(shared_acc[h][:, :], plain_w[:, TQ * k + t, :], moving,
                                             start=(n == row.n_open and k == 0 and t == 0),
                                             stop=(n == row.n - 1 and k == NQ - 1 and t == TQ - 1))
                    last.then_inc(adj_used, 1)

            def gates(row):
                for h in range(2):
                    pe.wait_ge(m_ready, 2 * row.index + h + 1)
                    pe.wait_ge(v_ready, 2 * row.index + h + 1)
                    if h == 0 and 0 < row.index <= NB:
                        pe.wait_ge(z_ready, row.index)
                    if h == 0 and row.index > NB:
                        pe.wait_ge(h_taken, row.q)
                    pe.matmul(rz_acc[h][:, :], w_rz[:, row.layer, :], gate_in[:, h, :], start=True, stop=True)
                    pe.matmul(n_acc[h][:, :], w_n[:, row.layer, :], gate_in[:, h, :],
                              start=True, stop=True).then_inc(gates_ready, 1)

            def make_z(row):
                pe.wait_ge(h_ready, h_count(row, 1))
                both = fresh[0:D, :, :].rearrange("d h n -> d (h n)")
                times_w(small_acc, lambda t: both[:, t * P:(t + 1) * P], 1).then_inc(z_product, 1)

            def turn(row):
                pe.wait_ge(h_ready, h_count(row, 1))
                both = fresh[0:D, :, :].rearrange("d h n -> d (h n)").rearrange("d (p i) -> d i p", i=KT)
                for i in range(KT):
                    last = pe.transpose(small_acc[:, i * D:(i + 1) * D], both[:, i, :], ident[:, :])
                last.then_inc(h_turned, 1)

            for row in rows:
                last_row = rows[row.index - 1] if row.index else None
                for n in range(row.peeled):
                    if row.is_open(n):
                        open_block(row, row.block0 + n, row.open0 + n, n)
                    else:
                        shared_block(row, row.block0 + n, row.shared0 + n - row.n_open, n)
                    if last_row and n == 0:
                        gates(last_row)
                    if last_row and n == min(2, row.n - 1) and row.n > 1:
                        if last_row.layer == 0:
                            make_z(last_row)
                        else:
                            turn(last_row)
                lo, hi = row.open_loop
                if hi - 1 > lo:
                    with pe.Fori(lo, hi - 1) as n:
                        open_block(row, row.block0 + n, row.open0 + n)
                if hi > lo:
                    open_block(row, row.block0 + hi - 1, row.open0 + hi - 1, hi - 1)
                lo, hi = row.shared_loop
                if hi > lo and lo == row.n_open:
                    shared_block(row, row.block0 + lo, row.shared0, lo)
                    lo += 1
                if hi - 1 > lo:
                    with pe.Fori(lo, hi - 1) as n:
                        shared_block(row, row.block0 + n, row.shared0 + n - row.n_open)
                if hi > lo:
                    shared_block(row, row.block0 + hi - 1, row.shared0 + hi - 1 - row.n_open, hi - 1)
            turn(rows[-2])
            gates(rows[-1])
            turn(rows[-1])


def kernel(**inputs):
    import numpy as np
    import concourse.bacc as bacc
    from concourse.bass_utils import run_bass_kernel_spmd as run

    def get(name):
        return np.asarray(inputs[name])

    adj = get("adj").reshape(NB, CH, NB, NQ, TQ, P).transpose(0, 2, 3, 5, 4, 1).reshape(NB, NB, NQ, P, TQ * CH)
    arrays = {"adj_t": np.ascontiguousarray(adj),
              "x_t": np.ascontiguousarray(get("x").T),
              "x": get("x").reshape(NB, P, KT * D)}
    for l in (1, 2):
        arrays[f"w{l}"] = get(f"L0_gnn_W{l}")
        arrays[f"wih_t{l}"] = np.ascontiguousarray(get(f"L0_gnn_wih{l}").T)
        arrays[f"whh_t{l}"] = np.ascontiguousarray(get(f"L0_gnn_whh{l}").T)
        arrays[f"bih{l}"] = get(f"L0_gnn_bih{l}")
        arrays[f"bhh{l}"] = get(f"L0_gnn_bhh{l}")

    nc = bacc.Bacc("TRN2", target_bir_lowering=False, num_devices=1)
    ap = {name: nc.dram_tensor(name, a.shape, mybir.dt.from_np(a.dtype), kind="ExternalInput").ap()
          for name, a in arrays.items()}
    out = nc.dram_tensor("out", (NB, P, KT * D), F32, kind="ExternalOutput").ap()
    gated_graph_layers(nc, ap["adj_t"], ap["x_t"], ap["x"], [ap["w1"], ap["w2"]],
                       [ap["wih_t1"], ap["wih_t2"]], [ap["whh_t1"], ap["whh_t2"]],
                       [ap["bih1"], ap["bih2"]], [ap["bhh1"], ap["bhh2"]], out)
    r = run(nc, [arrays], core_ids=[0])
    return r.results[0]["out"].reshape(N, D)
```

```python
import concourse.bass as bass
from concourse import mybir
from contextlib import ExitStack

F32 = mybir.dt.float32
F32R = mybir.dt.float32r
ACT = mybir.ActivationFunctionType
ALU = mybir.AluOpType
AX = mybir.AxisListType

N = 8192
D = 64
P = 128
CH = 1024
NB = N // CH
HALF = 512
KT = CH // P
NQ = 4
TQ = KT // NQ
SPLITS = 4
EPS = 1e-5


OPEN_SUM, SUM, GATES, SIGMOID, PRE_TANH, TANH, MIX, RELU, TURN, KEEP, NORM, SCALE = range(12)
AFTER_OPEN = {OPEN_SUM: 0}
AFTER_END = {SUM: 0}
AFTER_LATE = {GATES: 0, SIGMOID: 2, PRE_TANH: 3, TANH: 4, MIX: 4, RELU: 7, TURN: 7, KEEP: 10, NORM: 9, SCALE: 11}
PASS_2 = [0, 7, 1, 6, 2, 5, 3, 4]


class Row:

    def __init__(self, index, first_block, first_open, first_shared):
        self.index = index
        self.layer = index // NB
        self.seq = index % NB
        self.q = PASS_2[self.seq] if self.layer else self.seq
        n_open = NB - self.q
        n_shared = self.q if self.layer == 0 else 0
        self.n = n_open + n_shared
        self.n_shared = n_shared
        pairs = min(n_open, n_shared)
        self.order = "O" * (n_open - pairs) + "OS" * pairs + "S" * (n_shared - pairs)
        self.block0 = first_block
        self.open0 = first_open
        self.shared0 = first_shared
        self.first = {kind: self.order.find(kind) for kind in "OS"}
        self.last = {kind: self.order.rfind(kind) for kind in "OS"}
        self.open_end = first_block + self.last["O"] + 1

    def before(self, n, kind):
        return self.order[:n].count(kind)

    def runs(self, busy):
        alone = busy | set(self.first.values()) | set(self.last.values())
        n, out = 0, []
        while n < self.n:
            pattern, times = self.order[n], 1
            if n not in alone:
                for p in ("OS", "SO", "O", "S"):
                    m = 0
                    while self.order[n + len(p) * m:n + len(p) * (m + 1)] == p and \
                            not alone & set(range(n + len(p) * m, n + len(p) * (m + 1))):
                        m += 1
                    if m * len(p) > times * len(pattern) and m > 1:
                        pattern, times = p, m
            out.append((n, pattern, times))
            n += len(pattern) * times
        return out


def all_rows():
    rows, b, o, s = [], 0, 0, 0
    for index in range(2 * NB):
        row = Row(index, b, o, s)
        rows.append(row)
        b, o, s = b + row.n, o + row.order.count("O"), s + row.n_shared
    return rows


def step_places(rows):
    places, late = {}, 0
    for row in rows:
        end = NQ * (row.block0 + row.n)
        late = max(end, late + 8)
        for base, steps in ((NQ * row.open_end, AFTER_OPEN), (end, AFTER_END), (late, AFTER_LATE)):
            for step, after in steps.items():
                places.setdefault(base + after, []).append((row, step))
    for due in places.values():
        due.sort(key=lambda x: (x[0].index, x[1]))
    return places


def gated_graph_layers(nc, adj_t, x_t, x, w, wih_t, whh_t, bih, bhh, out):
    rows = all_rows()
    n_blocks = rows[-1].block0 + rows[-1].n
    places = step_places(rows)

    def work_through(engine, do_open, do_shared, steps):
        for row in rows:
            busy = {q // NQ - row.block0 for q in places}
            if row.index == 0:
                busy |= {0, 1, 2}
            for n0, pattern, times in row.runs(busy):
                def blocks(i, n):
                    for p, kind in enumerate(pattern):
                        before = row.before(n0, kind)
                        b = row.block0 + n0 + len(pattern) * i + p
                        if kind == "O":
                            do_open(row, b, row.open0 + before + i, row.q + before + i, n)
                        else:
                            do_shared(row, b, row.shared0 + before + i, before + i, n)
                if times == 1:
                    blocks(0, n0)
                else:
                    with engine.Fori(0, times) as i:
                        blocks(i, None)
        for quarter in range(NQ * n_blocks, max(places) + 1):
            steps(quarter)

    def due(quarter):
        return places.get(quarter, [])
    with ExitStack() as ctx:
        def sb(name, shape, dt=F32):
            return ctx.enter_context(nc.sbuf_tensor(name, shape, dt))

        def bank(name):
            return ctx.enter_context(nc.psum_tensor(name, [P, HALF], F32))

        def sem(name):
            return ctx.enter_context(nc.semaphore(name))

        adj_in = sb("adj_in", [P, 2 * NQ, TQ * CH])
        adj_hi = sb("adj_hi", [P, SPLITS, CH], F32R)
        adj_lo = sb("adj_lo", [P, SPLITS, CH], F32R)
        yz = sb("yz", [P, NB, KT, 2 * D])
        split_w = sb("split_w", [P, KT, 2 * D], F32R)
        plain_w = sb("plain_w", [P, KT, 2 * D])
        state = sb("state", [P, N])
        gate_in = sb("gate_in", [P, 2, HALF])
        rz = sb("rz", [P, 2, HALF])
        work = sb("work", [P, 2, HALF])
        fresh = sb("fresh", [P, 2, HALF])
        x_row = sb("x_row", [P, 2, KT * D])
        summed = sb("summed", [P, KT, D])
        squared = sb("squared", [P, KT, D])
        stats = sb("stats", [P, 4, KT])
        minus_half = sb("minus_half", [P, KT])
        w_in = sb("w_in", [D, 2, D])
        w_rz = sb("w_rz", [P, 2, P])
        w_n = sb("w_n", [P, 2, P])
        bias = sb("bias", [P, 2, 4])
        ident = sb("ident", [D, D])

        open_acc = [bank("open_acc0"), bank("open_acc1")]
        shared_acc = [bank("shared_acc0"), bank("shared_acc1")]
        rz_acc = [bank("rz_acc0"), bank("rz_acc1")]
        n_acc = [bank("n_acc0"), bank("n_acc1")]
        small_acc = rz_acc[0]

        x_first = sem("x_first")
        x_rest = sem("x_rest")
        x_copy = sem("x_copy")
        w_loaded = sem("w_loaded")
        adj_loaded = [sem(f"adj_loaded{k}") for k in range(NQ)]
        adj_used = sem("adj_used")
        hi_ready = sem("hi_ready")
        lo_ready = sem("lo_ready")
        split_hi = sem("split_hi")
        split_ready = sem("split_ready")
        plain_ready = sem("plain_ready")
        y_product = sem("y_product")
        y_ready = sem("y_ready")
        z_product = sem("z_product")
        z_ready = sem("z_ready")
        w_n_zero = sem("w_n_zero")
        bias_ready = sem("bias_ready")
        ident_ready = sem("ident_ready")
        low_part = sem("low_part")
        partial_saved = sem("partial_saved")
        open_summed = sem("open_summed")
        rest_summed = sem("rest_summed")
        v_ready = sem("v_ready")
        gates_ready = sem("gates_ready")
        rz_ready = sem("rz_ready")
        pre_ready = sem("pre_ready")
        n_ready = sem("n_ready")
        new_ready = sem("new_ready")
        h_ready = sem("h_ready")
        h_turned = sem("h_turned")
        h_taken = sem("h_taken")
        x_row_loaded = [sem("x_row_loaded0"), sem("x_row_loaded1")]
        var_ready = sem("var_ready")
        mean_ready = sem("mean_ready")
        squares_ready = sem("squares_ready")
        root_ready = sem("root_ready")
        norm_ready = sem("norm_ready")
        stored = sem("stored")
        dve_step = sem("dve_step")
        pool_step = sem("pool_step")

        block = ctx.enter_context(nc.Block())

        def ring(b, k):
            return (b % 2) * NQ + k

        def in_slot(b, k, cols=slice(0, TQ * CH)):
            return adj_in[:, ring(b, k), cols] if isinstance(b, int) else adj_in[:, bass.ds(ring(b, k), 1), cols]

        def in_tile(b, j, at=0, n=CH):
            at += j % TQ * CH
            return in_slot(b, j // TQ, slice(at, at + n))

        def chunk_w(c, tiles, cols):
            if isinstance(c, int):
                return yz[:, c, tiles, cols]
            return yz[:, bass.ds(c, 1), tiles, cols]

        def nodes(row, half):
            at = row.q * CH + half * HALF
            return slice(at, at + HALF)

        def h_count(row):
            return 4 * (row.seq + 1) if row.layer == 0 else 4 * NB + 2 * (row.seq + 1)

        def rest_count(row):
            return 2 * (row.index - 1 - row.layer) + 1

        def spread(column):
            return column.rearrange("p (t a) -> p t a", a=1).to_broadcast([P, KT, D])

        Y_GROUPS = [(0, 1), (2, 3, 4), (5, 6, 7)]
        Y_MADE = [NQ - 1, 2 * NQ - 1]
        Y_KEPT = [NQ + 2, 2 * NQ + 2]
        Y_ACC = [rz_acc[0], rz_acc[1], n_acc[0]]
        W_LOADS = 17

        def y_acc(c):
            return Y_ACC[c % len(Y_ACC)]

        @block.sync
        def _(sp):
            sp.dma_start(state[0:D, 0:2 * CH], x_t[:, 0:2 * CH]).then_inc(x_first, 16)
            sp.dma_start(w_in[:, 0, :], w[0]).then_inc(x_first, 16)
            loads_register = sp.alloc_register("loads")

            def load(row, b, c):
                loads = 16 * b
                used = [KT * (b - 2) + TQ * (k + 1) for k in range(NQ)]
                if not isinstance(b, int):
                    sp.reg_mov(loads_register, loads)
                    loads = sp.snap(loads_register)
                for k in range(NQ):
                    if not isinstance(b, int) or b >= 2:
                        sp.wait_ge(adj_used, used[k])
                    if not isinstance(b, int) or b >= 1:
                        sp.wait_ge(adj_loaded[k], loads)
                    src = adj_t[row.q, c, k, :, :] if isinstance(c, int) else adj_t[row.q, bass.ds(c, 1), k, :, :]
                    sp.dma_start(in_slot(b, k), src).then_inc(adj_loaded[k], 16)

            def load_block(row, b, i, c, n):
                load(row, b, c)
                if row.index == 0 and n == 0:
                    sp.dma_start(state[0:D, 2 * CH:N], x_t[:, 2 * CH:N]).then_inc(x_rest, 16)
                if row.index == 0 and n == 1:
                    sp.dma_start(state[D:P, :], x_t).then_inc(x_copy, 16)

            work_through(sp, load_block, load_block, lambda quarter: None)

        @block.scalar
        def _(act):
            def keep_y(c):
                act.wait_ge(y_product, c + 1)
                act.activation(yz[:, c, :, 0:D], y_acc(c)[:, :].rearrange("p (t d) -> p t d", d=D),
                               ACT.Copy).then_inc(y_ready, 1)

            for c in Y_GROUPS[0]:
                keep_y(c)

            def stage_hi(row, b, o, c, g):
                if not isinstance(b, int) or b >= 1:
                    act.wait_ge(adj_used, KT * b + 4 * g - 4)
                if row.layer == 0:
                    act.wait_ge(y_ready, c + 1)
                else:
                    act.wait_ge(z_ready, c + 1)
                tiles = slice(4 * g, 4 * g + 4)
                act.activation(split_w[:, tiles, 0:D], chunk_w(c, tiles, slice(row.layer * D, row.layer * D + D)),
                               ACT.Copy).then_inc(split_hi, 1)

            def tile_hi(b, j):
                if j % TQ == 0:
                    act.wait_ge(adj_loaded[j // TQ], 16 * (b + 1))
                if not isinstance(b, int) or KT * b + j >= SPLITS:
                    act.wait_ge(adj_used, KT * b + j - SPLITS + 1)
                act.activation(adj_hi[:, j % SPLITS, :], in_tile(b, j), ACT.Copy).then_inc(hi_ready, 1)

            def move_low(row):
                act.wait_ge(adj_used, KT * row.open_end)
                for h in range(2):
                    act.activation(work[0:D, h, :], open_acc[h][D:P, :], ACT.Copy).then_inc(low_part, 1)

            def save_partial(row):
                if row.n_shared:
                    act.wait_ge(adj_used, KT * (row.block0 + row.n))
                    for h in range(2):
                        act.activation(state[0:D, nodes(row, h)], shared_acc[h][D:P, :], ACT.Copy).then_inc(partial_saved, 1)

            def sigmoids(row):
                if row.index == 0:
                    act.wait_ge(bias_ready, 2)
                for h in range(2):
                    act.wait_ge(gates_ready, 2 * row.index + h + 1)
                    act.activation(rz[:, h, :], rz_acc[h][:, :], ACT.Sigmoid, bias=bias[:, row.layer, 3:4]).then_inc(rz_ready, 1)

            def tanhs(row):
                for h in range(2):
                    act.wait_ge(pre_ready, 2 * row.index + h + 1)
                    act.activation(fresh[D:P, h, :], work[D:P, h, :], ACT.Tanh, bias=bias[D:P, row.layer, 2:3]).then_inc(n_ready, 1)

            def relus(row):
                for h in range(2):
                    act.wait_ge(new_ready, 2 * row.index + h + 1)
                    if row.layer == 0:
                        act.activation(state[D:P, nodes(row, h)], gate_in[D:P, h, :], ACT.Relu).then_inc(h_ready, 1)
                    elif row.seq:
                        act.wait_ge(h_turned, row.seq)
                    act.activation(fresh[0:D, h, :], gate_in[D:P, h, :], ACT.Relu).then_inc(h_ready, 1)

            def keep_z(row):
                act.wait_ge(z_product, row.q + 1)
                act.activation(yz[:, row.q, :, D:P], small_acc[:, :].rearrange("p (t d) -> p t d", d=D),
                               ACT.Copy).then_inc(z_ready, 1)

            def open_block(row, b, o, c, n):
                for k in range(NQ):
                    if k % 2 == 0:
                        stage_hi(row, b, o, c, k // 2)
                    for j in range(TQ * k, TQ * (k + 1)):
                        tile_hi(b, j)
                    if n is not None:
                        steps(NQ * b + k)

            def shared_block(row, b, s, c, n):
                if n is not None:
                    for k in range(NQ):
                        steps(NQ * b + k)

            def steps(quarter):
                if quarter in Y_KEPT:
                    for c in Y_GROUPS[Y_KEPT.index(quarter) + 1]:
                        keep_y(c)
                for row, step in due(quarter):
                    if step == OPEN_SUM:
                        move_low(row)
                    if step == SUM:
                        save_partial(row)
                    if step == SIGMOID:
                        sigmoids(row)
                    if step == TANH:
                        tanhs(row)
                    if step == RELU:
                        relus(row)
                    if step == KEEP and row.layer == 0:
                        keep_z(row)

            work_through(act, open_block, shared_block, steps)

        @block.vector
        def _(dve):
            done = [0]

            def then_next(ins):
                done[0] += 1
                ins.then_inc(dve_step, 1)
                dve.wait_ge(dve_step, done[0])

            def stage_lo(row, o, c, g):
                dve.wait_ge(split_hi, 2 * o + g + 1)
                tiles = slice(4 * g, 4 * g + 4)
                dve.tensor_tensor(split_w[:, tiles, D:P], chunk_w(c, tiles, slice(row.layer * D, row.layer * D + D)),
                                  split_w[:, tiles, 0:D].bitcast(F32), ALU.subtract).then_inc(split_ready, 1)

            def tile_lo(b, o, j):
                dve.wait_ge(hi_ready, KT * o + j + 1)
                dve.tensor_tensor(adj_lo[:, j % SPLITS, :], in_tile(b, j), adj_hi[:, j % SPLITS, :].bitcast(F32),
                                  ALU.subtract).then_inc(lo_ready, 1)

            def sum_open(row):
                for h in range(2):
                    dve.wait_ge(low_part, 2 * row.index + h + 1)
                    dve.tensor_tensor(gate_in[0:D, h, :], open_acc[h][0:D, :], work[0:D, h, :],
                                      ALU.add).then_inc(open_summed, 1)

            def sum_rest(row):
                if row.q == 0:
                    return
                dve.wait_ge(adj_used, KT * (row.block0 + row.n))
                for h in range(2):
                    dve.wait_ge(open_summed, 2 * row.index + h + 1)
                    m = gate_in[0:D, h, :]
                    rest = shared_acc[h][0:D, :] if row.layer == 0 else state[0:D, nodes(row, h)]
                    dve.tensor_tensor(m, rest, m, ALU.add).then_inc(rest_summed, 1)

            def pre_tanh(row):
                for h in range(2):
                    dve.wait_ge(rz_ready, 2 * row.index + h + 1)
                    then_next(dve.scalar_tensor_tensor(out=work[D:P, h, :], in0=n_acc[h][0:D, :],
                                                       scalar=bias[0:D, row.layer, 2:3], in1=rz[0:D, h, :],
                                                       op0=ALU.add, op1=ALU.mult))
                    dve.tensor_tensor(work[D:P, h, :], n_acc[h][D:P, :], work[D:P, h, :], ALU.add).then_inc(pre_ready, 1)

            def add_x(row):
                dve.wait_ge(h_turned, row.seq + 1)
                dve.wait_ge(x_row_loaded[row.seq % 2], 16 * (row.seq // 2 + 1))
                if row.seq:
                    dve.wait_ge(stored, 16 * row.seq)
                dve.tensor_tensor(summed[:, :, :], small_acc[:, :].rearrange("p (t d) -> p t d", d=D),
                                  x_row[:, row.seq % 2, :].rearrange("p (t d) -> p t d", d=D), ALU.add).then_inc(h_taken, 1)
                dve.wait_ge(h_taken, row.seq + 1)
                dve.tensor_reduce(stats[:, 0, :], summed[:, :, :], AX.X, ALU.add).then_inc(mean_ready, 1)

            def variance(row):
                if row is rows[-1]:
                    dve.wait_ge(mean_ready, NB)
                    then_next(dve.tensor_scalar(stats[:, 1, :], stats[:, 0, :], 1.0 / D, None, ALU.mult))
                    then_next(dve.tensor_tensor(summed[:, :, :], summed[:, :, :], spread(stats[:, 1, :]), ALU.subtract))
                    then_next(dve.tensor_tensor(squared[:, :, :], summed[:, :, :], summed[:, :, :], ALU.mult))
                else:
                    dve.wait_ge(squares_ready, row.seq + 1)
                dve.tensor_reduce(stats[:, 2, :], squared[:, :, :], AX.X, ALU.add).then_inc(var_ready, 1)

            def scale_last():
                dve.wait_ge(root_ready, NB)
                dve.tensor_tensor(summed[:, :, :], summed[:, :, :], spread(stats[:, 0, :]), ALU.mult).then_inc(norm_ready, 1)

            def mix_last(row):
                for h in range(2):
                    v = gate_in[D:P, h, :]
                    dve.wait_ge(n_ready, 2 * row.index + h + 1)
                    then_next(dve.tensor_tensor(v, v, fresh[D:P, h, :], ALU.subtract))
                    then_next(dve.tensor_tensor(v, v, rz[D:P, h, :], ALU.mult))
                    dve.tensor_tensor(v, v, fresh[D:P, h, :], ALU.add).then_inc(new_ready, 1)

            def open_block(row, b, o, c, n):
                for k in range(NQ):
                    if k % 2 == 0:
                        stage_lo(row, o, c, k // 2)
                    for j in range(TQ * k, TQ * (k + 1)):
                        tile_lo(b, o, j)
                    if n is not None:
                        steps(NQ * b + k)

            def shared_block(row, b, s, c, n):
                if n is not None:
                    for k in range(NQ):
                        steps(NQ * b + k)

            def steps(quarter):
                for row, step in due(quarter):
                    if step == OPEN_SUM:
                        sum_open(row)
                    if step == SUM:
                        sum_rest(row)
                    if step == PRE_TANH:
                        pre_tanh(row)
                    if step == MIX and row is rows[-1]:
                        mix_last(row)
                    if step == NORM and row.layer == 1:
                        add_x(row)
                    if step == SCALE and row.layer == 1:
                        variance(row)
                    if step == SCALE and row is rows[-1]:
                        scale_last()

            work_through(dve, open_block, shared_block, steps)

        @block.gpsimd
        def _(pool):
            done = [0]

            def then_next(ins):
                done[0] += 1
                ins.then_inc(pool_step, 1)
                pool.wait_ge(pool_step, done[0])

            then_next(pool.memset(w_n[:, :, :], 0.0))
            for l in range(2):
                if l:
                    pool.dma_start(w_in[:, l, :], w[l]).then_inc(w_loaded, 16)
                for part, weights, other in ((slice(0, D), wih_t[l], slice(D, P)), (slice(D, P), whh_t[l], slice(0, D))):
                    pool.dma_start(w_rz[part, l, :], weights[:, 0:P]).then_inc(w_loaded, 16)
                    pool.dma_start(w_n[part, l, other], weights[:, P:3 * D]).then_inc(w_loaded, 16)
                for col, vec in ((0, bih), (1, bhh)):
                    pool.dma_start(bias[:, l, col:col + 1], vec[l][0:P].rearrange("(p a) -> p a", a=1)).then_inc(w_loaded, 16)
                pool.dma_start(bias[0:D, l, 2:3], bhh[l][P:3 * D].rearrange("(p a) -> p a", a=1)).then_inc(w_loaded, 16)
                pool.dma_start(bias[D:P, l, 2:3], bih[l][P:3 * D].rearrange("(p a) -> p a", a=1)).then_inc(w_loaded, 16)
            then_next(pool.memset(minus_half[:, :], -0.5))
            then_next(pool.memset(ident[:, :], 0.0))
            pool.affine_select(out=ident[:, :], in_=ident[:, :], compare_op=ALU.not_equal, fill=1.0, base=0,
                               pattern=[[-1, D]], channel_multiplier=1).then_inc(ident_ready, 1)
            pool.wait_ge(ident_ready, 1)
            pool.wait_ge(w_loaded, 16 * W_LOADS)
            for l in range(2):
                pool.tensor_tensor(bias[:, l, 3:4], bias[:, l, 0:1], bias[:, l, 1:2], ALU.add).then_inc(bias_ready, 1)
            pool.wait_ge(bias_ready, 2)

            def shared_block(row, b, s, c, n):
                for g in range(2):
                    pool.wait_ge(adj_used, KT * b + 4 * g - 4)
                    pool.wait_ge(z_ready, c + 1)
                    tiles = slice(4 * g, 4 * g + 4)
                    pool.tensor_copy(plain_w[:, tiles, :], chunk_w(c, tiles, slice(0, P))).then_inc(plain_ready, 1)
                if n is not None:
                    for k in range(NQ):
                        steps(NQ * b + k)

            def open_block(row, b, o, c, n):
                if n is not None:
                    for k in range(NQ):
                        steps(NQ * b + k)

            def stages_done(quarter):
                b = min(quarter // NQ, n_blocks - 1)
                row = [row for row in rows if row.block0 <= b][-1]
                count = 2 * (row.shared0 + row.before(b - row.block0 + 1, "S"))
                if count:
                    pool.wait_ge(plain_ready, count)

            def copy_v(row):
                for h in range(2):
                    if row.index == 0:
                        pool.wait_ge(x_copy, 16)
                    else:
                        pool.wait_ge(h_ready, h_count(rows[row.index - 1]))
                    if row.layer:
                        pool.wait_ge(h_ready, h_count(rows[row.q]))
                    ins = pool.tensor_copy(gate_in[D:P, h, :], state[D:P, nodes(row, h)])
                    ins.then_inc(v_ready, 1)
                pool.wait_ge(v_ready, 2 * row.index + 2)

            def mix(row):
                for h in range(2):
                    v = gate_in[D:P, h, :]
                    pool.wait_ge(n_ready, 2 * row.index + h + 1)
                    then_next(pool.tensor_tensor(v, v, fresh[D:P, h, :], ALU.subtract))
                    then_next(pool.tensor_tensor(v, v, rz[D:P, h, :], ALU.mult))
                    pool.tensor_tensor(v, v, fresh[D:P, h, :], ALU.add).then_inc(new_ready, 1)
                pool.wait_ge(new_ready, 2 * row.index + 2)

            def load_x(row):
                if row.seq >= 2:
                    pool.wait_ge(h_taken, row.seq - 1)
                pool.dma_start(x_row[:, row.seq % 2, :], x[row.q]).then_inc(x_row_loaded[row.seq % 2], 16)

            def center(row):
                pool.wait_ge(mean_ready, row.seq + 1)
                then_next(pool.tensor_scalar(stats[:, 1, :], stats[:, 0, :], 1.0 / D, None, ALU.mult))
                then_next(pool.tensor_tensor(summed[:, :, :], summed[:, :, :], spread(stats[:, 1, :]), ALU.subtract))
                pool.tensor_tensor(squared[:, :, :], summed[:, :, :], summed[:, :, :], ALU.mult).then_inc(squares_ready, 1)

            def scale(row):
                pool.wait_ge(var_ready, row.seq + 1)
                then_next(pool.tensor_scalar(stats[:, 3, :], stats[:, 2, :], 1.0 / D, EPS, ALU.mult, ALU.add))
                pool.tensor_tensor(stats[:, 0, :], stats[:, 3, :], minus_half[:, :], ALU.pow).then_inc(root_ready, 1)
                pool.wait_ge(root_ready, row.seq + 1)
                if row is not rows[-1]:
                    pool.tensor_tensor(summed[:, :, :], summed[:, :, :], spread(stats[:, 0, :]), ALU.mult).then_inc(norm_ready, 1)
                pool.wait_ge(norm_ready, row.seq + 1)
                pool.dma_start(out[row.q], summed[:, :, :].rearrange("p t d -> p (t d)")).then_inc(stored, 16)

            def steps(quarter):
                for row, step in due(quarter):
                    if step in (SUM, MIX, NORM):
                        stages_done(quarter)
                    if step == SUM:
                        copy_v(row)
                        if row.layer:
                            load_x(row)
                    if step == MIX and row is not rows[-1]:
                        mix(row)
                    if step == NORM and row.layer == 1 and row is not rows[-1]:
                        center(row)
                    if step == SCALE and row.layer == 1:
                        scale(row)

            work_through(pool, open_block, shared_block, steps)
            pool.wait_ge(stored, 16 * NB)

        @block.tensor
        def _(pe):
            def times_w(acc, source, l):
                for t in range(KT):
                    last = pe.matmul(acc[:, t * D:(t + 1) * D], source(t), w_in[:, l, :], start=True, stop=True)
                return last

            def make_y(group):
                for c in group:
                    if c >= len(Y_ACC):
                        pe.wait_ge(y_ready, c - len(Y_ACC) + 1)
                    times_w(y_acc(c), lambda t: state[0:D, c * CH + t * P:c * CH + (t + 1) * P], 0).then_inc(y_product, 1)

            pe.wait_ge(x_first, 32)
            make_y(Y_GROUPS[0])

            def free_acc(row, n):
                if n == 0 and row.index:
                    pe.wait_ge(open_summed, 2 * row.index)
                if n == row.first["S"] and row.q > 1:
                    pe.wait_ge(rest_summed, rest_count(row) - 1)
                    pe.wait_ge(partial_saved, 2 * (row.q - 1))

            def open_block(row, b, o, c, n):
                free_acc(row, n)
                for j in range(KT):
                    if j % 4 == 0:
                        pe.wait_ge(split_ready, 2 * o + j // 4 + 1)
                    pe.wait_ge(lo_ready, KT * o + j + 1)
                    for part in (adj_hi, adj_lo):
                        for h in range(2):
                            last = pe.matmul(open_acc[h][:, :], split_w[:, j, :],
                                             part[:, j % SPLITS, h * HALF:(h + 1) * HALF],
                                             start=(n == 0 and j == 0 and part is adj_hi),
                                             stop=(n == row.last["O"] and j == KT - 1 and part is adj_lo))
                    last.then_inc(adj_used, 1)
                    if n is not None and j % TQ == TQ - 1:
                        steps(NQ * b + j // TQ)

            def shared_block(row, b, s, c, n):
                free_acc(row, n)
                for j in range(KT):
                    if j % 4 == 0:
                        pe.wait_ge(plain_ready, 2 * s + j // 4 + 1)
                    if j % TQ == 0:
                        pe.wait_ge(adj_loaded[j // TQ], 16 * (b + 1))
                    for h in range(2):
                        last = pe.matmul(shared_acc[h][:, :], plain_w[:, j, :], in_tile(b, j, h * HALF, HALF),
                                         start=(n == row.first["S"] and j == 0), stop=(n == row.last["S"] and j == KT - 1))
                    last.then_inc(adj_used, 1)
                    if n is not None and j % TQ == TQ - 1:
                        steps(NQ * b + j // TQ)

            def gates(row):
                if row.index == 0:
                    pe.wait_ge(w_loaded, 16 * W_LOADS)
                for h in range(2):
                    pe.wait_ge(open_summed, 2 * row.index + h + 1)
                    if row.q:
                        pe.wait_ge(rest_summed, rest_count(row) + h)
                    pe.wait_ge(v_ready, 2 * row.index + h + 1)
                    if h == 0 and 0 < row.index <= NB:
                        pe.wait_ge(z_ready, row.index)
                    if h == 0 and row.index > NB:
                        pe.wait_ge(h_taken, row.seq)
                    pe.matmul(rz_acc[h][:, :], w_rz[:, row.layer, :], gate_in[:, h, :], start=True, stop=True)
                    pe.matmul(n_acc[h][:, :], w_n[:, row.layer, :], gate_in[:, h, :],
                              start=True, stop=True).then_inc(gates_ready, 1)

            def make_z(row):
                pe.wait_ge(h_ready, h_count(row))
                both = fresh[0:D, :, :].rearrange("d h n -> d (h n)")
                times_w(small_acc, lambda t: both[:, t * P:(t + 1) * P], 1).then_inc(z_product, 1)

            def turn(row):
                if row.seq == 0:
                    pe.wait_ge(ident_ready, 1)
                pe.wait_ge(h_ready, h_count(row))
                both = fresh[0:D, :, :].rearrange("d h n -> d (h n)").rearrange("d (p i) -> d i p", i=KT)
                for i in range(KT):
                    last = pe.transpose(small_acc[:, i * D:(i + 1) * D], both[:, i, :], ident[:, :])
                last.then_inc(h_turned, 1)

            def steps(quarter):
                if quarter in Y_MADE:
                    if quarter == Y_MADE[0]:
                        pe.wait_ge(x_rest, 16)
                    make_y(Y_GROUPS[Y_MADE.index(quarter) + 1])
                for row, step in due(quarter):
                    if step == GATES:
                        gates(row)
                    if step == TURN and row.layer == 0:
                        make_z(row)
                    if step == TURN and row.layer == 1:
                        turn(row)

            work_through(pe, open_block, shared_block, steps)


def kernel(**inputs):
    import numpy as np
    import concourse.bacc as bacc
    from concourse.bass_utils import run_bass_kernel_spmd as run

    def get(name):
        return np.asarray(inputs[name])

    adj = get("adj").reshape(NB, CH, NB, NQ, TQ, P).transpose(0, 2, 3, 5, 4, 1).reshape(NB, NB, NQ, P, TQ * CH)
    arrays = {"adj_t": np.ascontiguousarray(adj),
              "x_t": np.ascontiguousarray(get("x").T),
              "x": get("x").reshape(NB, P, KT * D)}
    for l in (1, 2):
        arrays[f"w{l}"] = get(f"L0_gnn_W{l}")
        arrays[f"wih_t{l}"] = np.ascontiguousarray(get(f"L0_gnn_wih{l}").T)
        arrays[f"whh_t{l}"] = np.ascontiguousarray(get(f"L0_gnn_whh{l}").T)
        arrays[f"bih{l}"] = get(f"L0_gnn_bih{l}")
        arrays[f"bhh{l}"] = get(f"L0_gnn_bhh{l}")

    nc = bacc.Bacc("TRN2", target_bir_lowering=False, num_devices=1)
    ap = {name: nc.dram_tensor(name, a.shape, mybir.dt.from_np(a.dtype), kind="ExternalInput").ap()
          for name, a in arrays.items()}
    out = nc.dram_tensor("out", (NB, P, KT * D), F32, kind="ExternalOutput").ap()
    gated_graph_layers(nc, ap["adj_t"], ap["x_t"], ap["x"], [ap["w1"], ap["w2"]],
                       [ap["wih_t1"], ap["wih_t2"]], [ap["whh_t1"], ap["whh_t2"]],
                       [ap["bih1"], ap["bih2"]], [ap["bhh1"], ap["bhh2"]], out)
    r = run(nc, [arrays], core_ids=[0])
    return r.results[0]["out"].reshape(N, D)
```

```python
import concourse.bass as bass
from concourse import mybir
from collections import namedtuple
from contextlib import ExitStack

F32 = mybir.dt.float32
F32R = mybir.dt.float32r
ACT = mybir.ActivationFunctionType
ALU = mybir.AluOpType
AX = mybir.AxisListType

N = 8192
D = 64
P = 128
CH = 1024
NB = N // CH
HALF = 512
KT = CH // P
NQ = 4
TQ = KT // NQ
EPS = 1e-5


(HELD_SUM, OPEN_SUM, SUM, GATES, SIGMOID, PRE_TANH, TANH, MIX, RELU, TURN, KEEP, NORM, SCALE) = range(13)
AFTER_LATE = [{GATES: 0, SIGMOID: 2, PRE_TANH: 3, TANH: 4, MIX: 4, RELU: 7, TURN: 7, KEEP: 10},
              {GATES: 0, SIGMOID: 3, PRE_TANH: 4, TANH: 5, MIX: 5, RELU: 8, TURN: 9, NORM: 11, SCALE: 13}]
APART = [8, 10]
PASS_2 = [0, 7, 1, 6, 2, 5, 3, 4]
HELD_AT = 3
PASS_1 = ["OOOOOOOD", "OOOHOOODS", "OOOHOSODS", "OOSHOSODS", "OSOHSOSDS", "OSOHSSSDS", "OSSHSSSDS", "ESSHSESSESDS"]
N_EARLY = PASS_1[-1].count("E")


class Block(namedtuple("Block", "kind n w r l o s c slot_was split_was plain_was")):

    def moving(self, later, i):
        return Block(self.kind, None, *[a if a == b else a + i if b == a + 1 else a + (b - a) * i
                                        for a, b in zip(self[2:], later[2:])])

    def steady(self, later, last, rounds):
        return all(z == a if a == b else a is not None and z == a + (b - a) * rounds
                   for a, b, z in zip(self[2:], later[2:], last[2:]))


class Row:

    def __init__(self, index, counts):
        self.index = index
        self.layer = index // NB
        self.seq = index % NB
        self.q = PASS_2[self.seq] if self.layer else self.seq
        self.n_shared = 0 if self.layer else self.q
        early = N_EARLY if index == NB else 0
        order = "O" * (NB - 1 - self.q - early) if self.layer else PASS_1[self.q]
        if index == NB:
            order = order[:HELD_AT] + "H" + order[HELD_AT:]
        self.order = order
        next_chunk = {"O": self.q + 1 + early, "D": self.q, "S": 0, "H": NB - 1 if self.layer else self.q - 1,
                      "E": PASS_2[0] + 1}
        self.blocks = []
        self.w0 = counts["w"]
        for n, kind in enumerate(order):
            w, ring = counts["w"], counts["ring"]
            self.blocks.append(Block(kind, n, w=w, r=len(ring), l=counts["l"], o=counts["o"], s=counts["s"],
                                     c=next_chunk[kind], slot_was=ring[-2] if len(ring) > 1 else None,
                                     split_was=counts["split"], plain_was=counts["plain"]))
            next_chunk[kind] += 1
            counts["w"] += 1
            counts["l"] += kind in "OSE"
            counts["o"] += kind in "ODHE"
            counts["s"] += kind == "S"
            if kind != "H":
                ring.append(w)
            counts["plain" if kind == "S" else "split"] = w
        self.end = counts["w"]
        opens = [b for b in self.blocks if b.kind in "OD"]
        shared = [b for b in self.blocks if b.kind == "S"]
        self.first_open, self.last_open = (opens[0].n, opens[-1].n) if opens else (None, None)
        if early:
            self.first_open = None
        self.first_early = order.index("E") if "E" in order else None
        self.first_shared, self.last_shared = (shared[0].n, shared[-1].n) if shared else (None, None)
        self.open_end = opens[-1].w + 1 if opens else None
        self.summed_before = counts["summed"]
        counts["summed"] += bool(opens)

    def runs(self, alone):
        alone = alone | {self.first_early, self.first_open, self.last_open, self.first_shared, self.last_shared}
        alone |= {b.n for b in self.blocks if b.kind in "DH"}
        n, out = 0, []
        while n < len(self.order):
            pattern, times = self.order[n], 1
            for p in ("OS", "SO", "O", "S", "E"):
                m = 0
                while self.order[n + len(p) * m:n + len(p) * (m + 1)] == p and \
                        not alone & set(range(n + len(p) * m, n + len(p) * (m + 1))) and \
                        all(m == 0 or self.blocks[k].steady(self.blocks[k + len(p)], self.blocks[k + m * len(p)], m)
                            for k in range(n, n + len(p))):
                    m += 1
                if m * len(p) > times * len(pattern) and m > 1:
                    pattern, times = p, m
            out.append((n, pattern, times))
            n += len(pattern) * times
        return out


def all_rows():
    counts = dict(w=0, ring=[], l=0, o=0, s=0, summed=0, split=None, plain=None)
    return [Row(index, counts) for index in range(2 * NB)]


def step_places(rows):
    places, late = {}, 0
    for row in rows:
        end = NQ * row.end
        late = max(end, late + APART[row.layer])
        at = {step: late + after for step, after in AFTER_LATE[row.layer].items()}
        at[SUM] = end if row.blocks else late
        if row.open_end:
            at[OPEN_SUM] = NQ * row.open_end
        if row.layer == 0:
            held = [b for b in rows[row.index + 1].blocks if b.kind == "H"][0]
            at[HELD_SUM] = NQ * (held.w + 1)
        for step, quarter in at.items():
            places.setdefault(quarter, []).append((row, step))
    for due in places.values():
        due.sort(key=lambda x: (x[0].index, x[1]))
    return places


def gated_graph_layers(nc, adj_t, x_t, x, w, wih_t, whh_t, bih, bhh, h_rows, part_rows, out):
    rows = all_rows()
    places = step_places(rows)
    held_block = {row.index - 1: b for row in rows for b in row.blocks if b.kind == "H"}

    def work_through(engine, visit, steps):
        for row in rows:
            single = {q // NQ - row.w0 for q in places}
            if row.index == 0:
                single |= {0, 1, 2}
            for n0, pattern, times in row.runs(single):
                if times == 1:
                    visit(row, row.blocks[n0])
                else:
                    with engine.Fori(0, times) as i:
                        for p in range(len(pattern)):
                            visit(row, row.blocks[n0 + p].moving(row.blocks[n0 + p + len(pattern)], i))
        for quarter in range(NQ * rows[-1].end, max(places) + 1):
            steps(quarter)

    def due(quarter):
        return places.get(quarter, [])

    with ExitStack() as ctx:
        def sb(name, shape, dt=F32):
            return ctx.enter_context(nc.sbuf_tensor(name, shape, dt))

        def two_views(name, shape):
            align = 32
            at = (nc.sbuf_base + align - 1) // align * align
            return sb(name, shape), nc.alloc_sbuf_tensor_at(name + "_low", shape, F32R, offset=at)

        def bank(name):
            return ctx.enter_context(nc.psum_tensor(name, [P, HALF], F32))

        def sem(name):
            return ctx.enter_context(nc.semaphore(name))

        (adj_in, adj_in_low), (held, held_low) = [
            two_views(name, shape) for name, shape in (
                ("adj_in", [P, 2 * NQ, TQ * CH]),
                ("held", [P, NQ, TQ * CH]))]
        adj_hi = sb("adj_hi", [P, KT, CH], F32R)
        yz = sb("yz", [P, NB, KT, 2 * D])
        split_w = sb("split_w", [P, KT, 2 * D], F32R)
        plain_w = sb("plain_w", [P, KT, 2 * D])
        part = sb("part", [D, 2, HALF])
        gate_in = sb("gate_in", [P, 2, HALF])
        rz = sb("rz", [P, 2, HALF])
        work = sb("work", [P, 2, HALF])
        fresh = sb("fresh", [P, 2, HALF])
        x_row = sb("x_row", [P, 2, KT * D])
        summed = sb("summed", [P, KT, D])
        squared = sb("squared", [P, KT, D])
        stats = sb("stats", [P, 4, KT])
        minus_half = sb("minus_half", [P, KT])
        w_in = sb("w_in", [D, 2, D])
        w_rz = sb("w_rz", [P, 2, P])
        w_n = sb("w_n", [P, 2, P])
        bias = sb("bias", [P, 2, 4])
        ident = sb("ident", [D, D])

        open_acc = [bank("open_acc0"), bank("open_acc1")]
        shared_acc = [bank("shared_acc0"), bank("shared_acc1")]
        rz_acc = [bank("rz_acc0"), bank("rz_acc1")]
        n_acc = [bank("n_acc0"), bank("n_acc1")]
        small_acc = rz_acc[0]

        x_first = sem("x_first")
        x_rest = sem("x_rest")
        w_loaded = sem("w_loaded")
        adj_loaded = [sem(f"adj_loaded{k}") for k in range(NQ)]
        held_loaded = [sem(f"held_loaded{k}") for k in range(NQ)]
        adj_used = sem("adj_used")
        hi_ready = sem("hi_ready")
        lo_ready = sem("lo_ready")
        split_hi = sem("split_hi")
        split_ready = sem("split_ready")
        plain_ready = sem("plain_ready")
        y_product = sem("y_product")
        y_ready = sem("y_ready")
        z_product = sem("z_product")
        z_ready = sem("z_ready")
        bias_ready = sem("bias_ready")
        ident_ready = sem("ident_ready")
        low_part = sem("low_part")
        partial_saved = sem("partial_saved")
        held_low_kept = sem("held_low_kept")
        held_summed = sem("held_summed")
        part_stored = sem("part_stored")
        part_loaded = sem("part_loaded")
        h_stored = sem("h_stored")
        open_summed = sem("open_summed")
        rest_summed = sem("rest_summed")
        v_ready = sem("v_ready")
        gates_ready = sem("gates_ready")
        rz_ready = sem("rz_ready")
        pre_ready = sem("pre_ready")
        n_ready = sem("n_ready")
        new_ready = sem("new_ready")
        h_ready = sem("h_ready")
        h_turned = sem("h_turned")
        h_taken = sem("h_taken")
        x_row_loaded = [sem("x_row_loaded0"), sem("x_row_loaded1")]
        var_ready = sem("var_ready")
        mean_ready = sem("mean_ready")
        squares_ready = sem("squares_ready")
        root_ready = sem("root_ready")
        norm_ready = sem("norm_ready")
        stored = sem("stored")
        last_stored = sem("last_stored")
        dve_step = sem("dve_step")
        pool_step = sem("pool_step")

        block = ctx.enter_context(nc.Block())

        def static(value):
            return isinstance(value, int)

        def in_slot(r, k, cols=slice(0, TQ * CH), view=None):
            view = view or adj_in
            slot = (r % 2) * NQ + k
            return view[:, slot, cols] if static(r) else view[:, bass.ds(slot, 1), cols]

        def in_tile(b, j, at=0, n=CH):
            at += j % TQ * CH
            if b.kind in "DH":
                return held[:, j // TQ, at:at + n]
            return in_slot(b.r, j // TQ, slice(at, at + n))

        def low_tile(b, j, at=0, n=CH):
            at += j % TQ * CH
            if b.kind == "H":
                return held_low[:, j // TQ, at:at + n]
            return in_slot(b.r, j // TQ, slice(at, at + n), adj_in_low)

        def chunk_w(c, tiles, cols):
            return yz[:, c, tiles, cols] if static(c) else yz[:, bass.ds(c, 1), tiles, cols]

        def open_banks(row):
            return n_acc if row.first_early is not None else open_acc

        def rest_count(row):
            return 2 * (row.index - 1) + 1

        def spread(column):
            return column.rearrange("p (t a) -> p t a", a=1).to_broadcast([P, KT, D])

        Y_CHUNKS = [(i + 1) % NB for i in range(NB)]
        Y_GROUPS = [(0, 1), (2, 3, 4), (5, 6, 7)]
        Y_MADE = [NQ - 1, 2 * NQ - 1]
        Y_KEPT = [NQ + 2, 2 * NQ + 2]
        Y_ACC = [rz_acc[0], rz_acc[1], n_acc[0]]
        x_chunk = [t[0:D, :, :].rearrange("p a n -> p (a n)") for t in (gate_in, rz, work, fresh, x_row, part, plain_w)]
        x_chunk.append(held[0:D, 0, 0:CH])
        W_LOADS = 17

        def y_acc(i):
            return Y_ACC[i % len(Y_ACC)]

        @block.sync
        def _(sp):
            def load_x_chunk(i, sem):
                c = Y_CHUNKS[i]
                sp.dma_start(x_chunk[i], x_t[:, c * CH:(c + 1) * CH]).then_inc(sem, 16)

            for i in Y_GROUPS[0]:
                load_x_chunk(i, x_first)
            sp.dma_start(w_in[:, 0, :], w[0]).then_inc(x_first, 16)
            loads_register = sp.alloc_register("loads")

            def load_block(row, b):
                if b.kind == "H":
                    return
                if b.kind == "D":
                    if row.index == 0:
                        sp.wait_ge(y_product, NB)
                    for k in range(NQ):
                        if row.index:
                            sp.wait_ge(adj_used, KT * held_block[row.index - 1].w + TQ * (k + 1))
                        sp.dma_start(held[:, k, :], adj_t[row.q, row.q, k, :, :]).then_inc(held_loaded[k], 16)
                    return
                loads = 16 * b.l
                if not static(b.l):
                    sp.reg_mov(loads_register, loads)
                    loads = sp.snap(loads_register)
                for k in range(NQ):
                    if b.slot_was is not None:
                        sp.wait_ge(adj_used, KT * b.slot_was + TQ * (k + 1))
                    if not static(b.l) or b.l >= 1:
                        sp.wait_ge(adj_loaded[k], loads)
                    q = PASS_2[0] if b.kind == "E" else row.q
                    src = adj_t[q, b.c, k, :, :] if static(b.c) else adj_t[q, bass.ds(b.c, 1), k, :, :]
                    sp.dma_start(in_slot(b.r, k), src).then_inc(adj_loaded[k], 16)
                if row.index == 0 and b.n == 0:
                    for i in Y_GROUPS[1] + Y_GROUPS[2]:
                        load_x_chunk(i, x_rest)

            work_through(sp, load_block, lambda quarter: None)
            sp.wait_ge(norm_ready, NB)
            sp.dma_start(out[rows[-1].q], summed[:, :, :].rearrange("p t d -> p (t d)")).then_inc(last_stored, 16)
            sp.wait_ge(last_stored, 16)
            sp.wait_ge(stored, 16 * (NB - 1))
            sp.wait_ge(h_stored, 16 * NB)
            sp.wait_ge(part_stored, 16 * NB)

        @block.scalar
        def _(act):
            def keep_y(i):
                act.wait_ge(y_product, i + 1)
                act.activation(yz[:, Y_CHUNKS[i], :, 0:D], y_acc(i)[:, :].rearrange("p (t d) -> p t d", d=D),
                               ACT.Copy).then_inc(y_ready, 1)

            for i in Y_GROUPS[0]:
                keep_y(i)

            def stage_hi(row, b, g):
                if b.split_was is not None:
                    act.wait_ge(adj_used, KT * b.split_was + 4 * g + 4)
                of_z = row.layer == 1 or b.kind in "HE"
                if of_z:
                    act.wait_ge(z_ready, b.c + 1)
                elif row.index == 0 and b.kind == "O":
                    act.wait_ge(y_ready, b.c)
                else:
                    act.wait_ge(y_ready, NB)
                tiles = slice(4 * g, 4 * g + 4)
                act.activation(split_w[:, tiles, 0:D], chunk_w(b.c, tiles, slice(of_z * D, of_z * D + D)),
                               ACT.Copy).then_inc(split_hi, 1)

            def tile_hi(row, b, j):
                if j % TQ == 0 and b.kind in "OE":
                    act.wait_ge(adj_loaded[j // TQ], 16 * (b.l + 1))
                if j % TQ == 0 and b.kind == "D":
                    act.wait_ge(held_loaded[j // TQ], 16 * (row.index + 1))
                act.activation(adj_hi[:, j, :], in_tile(b, j), ACT.Copy).then_inc(hi_ready, 1)

            def move_held(row):
                act.wait_ge(adj_used, KT * (held_block[row.index].w + 1))
                for h in range(2):
                    act.activation(work[0:D, h, :], n_acc[h][D:P, :], ACT.Copy).then_inc(held_low_kept, 1)

            def move_low(row):
                act.wait_ge(adj_used, KT * row.open_end)
                if row.summed_before:
                    act.wait_ge(open_summed, 2 * row.summed_before)
                if row.index:
                    act.wait_ge(held_summed, 2 * min(row.index, NB))
                for h in range(2):
                    act.activation(work[0:D, h, :], open_banks(row)[h][D:P, :], ACT.Copy).then_inc(low_part, 1)

            def save_partial(row):
                if row.n_shared:
                    act.wait_ge(adj_used, KT * row.end)
                    act.wait_ge(part_stored, 16 * row.index)
                    for h in range(2):
                        act.activation(part[:, h, :], shared_acc[h][D:P, :], ACT.Copy).then_inc(partial_saved, 1)

            def sigmoids(row):
                if row.index == 0:
                    act.wait_ge(bias_ready, 2)
                for h in range(2):
                    act.wait_ge(gates_ready, 2 * row.index + h + 1)
                    act.activation(rz[:, h, :], rz_acc[h][:, :], ACT.Sigmoid, bias=bias[:, row.layer, 3:4]).then_inc(rz_ready, 1)

            def tanhs(row):
                for h in range(2):
                    act.wait_ge(pre_ready, 2 * row.index + h + 1)
                    act.activation(fresh[D:P, h, :], work[D:P, h, :], ACT.Tanh, bias=bias[D:P, row.layer, 2:3]).then_inc(n_ready, 1)

            def relus(row):
                if row.index:
                    act.wait_ge(h_stored, 16 * min(row.index, NB))
                if row.layer and row.seq:
                    act.wait_ge(h_turned, row.seq)
                for h in range(2):
                    act.wait_ge(new_ready, 2 * row.index + h + 1)
                    act.activation(fresh[0:D, h, :], gate_in[D:P, h, :], ACT.Relu).then_inc(h_ready, 1)

            def keep_z(row):
                act.wait_ge(z_product, row.q + 1)
                act.activation(yz[:, row.q, :, D:P], small_acc[:, :].rearrange("p (t d) -> p t d", d=D),
                               ACT.Copy).then_inc(z_ready, 1)

            def block_hi(row, b):
                for k in range(NQ):
                    if b.kind != "S":
                        if k % 2 == 0:
                            stage_hi(row, b, k // 2)
                        for j in range(TQ * k, TQ * (k + 1)):
                            tile_hi(row, b, j)
                    if b.n is not None:
                        steps(NQ * b.w + k)

            def steps(quarter):
                if quarter in Y_KEPT:
                    for i in Y_GROUPS[Y_KEPT.index(quarter) + 1]:
                        keep_y(i)
                for row, step in due(quarter):
                    if step == HELD_SUM:
                        move_held(row)
                    if step == OPEN_SUM:
                        move_low(row)
                    if step == SUM:
                        save_partial(row)
                    if step == SIGMOID:
                        sigmoids(row)
                    if step == TANH:
                        tanhs(row)
                    if step == RELU:
                        relus(row)
                    if step == KEEP and row.layer == 0:
                        keep_z(row)

            work_through(act, block_hi, steps)

        @block.vector
        def _(dve):
            done = [0]

            def then_next(ins):
                done[0] += 1
                ins.then_inc(dve_step, 1)
                dve.wait_ge(dve_step, done[0])

            def stage_lo(row, b, g):
                dve.wait_ge(split_hi, 2 * b.o + g + 1)
                tiles = slice(4 * g, 4 * g + 4)
                of_z = row.layer == 1 or b.kind in "HE"
                dve.tensor_tensor(split_w[:, tiles, D:P], chunk_w(b.c, tiles, slice(of_z * D, of_z * D + D)),
                                  split_w[:, tiles, 0:D].bitcast(F32), ALU.subtract).then_inc(split_ready, 1)

            def tile_lo(b, j):
                dve.wait_ge(hi_ready, KT * b.o + j + 1)
                if b.kind == "D" and j % TQ == 0:
                    dve.wait_ge(adj_used, KT * b.slot_was + j + TQ)
                dve.tensor_tensor(low_tile(b, j), in_tile(b, j), adj_hi[:, j, :].bitcast(F32),
                                  ALU.subtract).then_inc(lo_ready, 1)

            def sum_held(row):
                for h in range(2):
                    dve.wait_ge(held_low_kept, 2 * row.index + h + 1)
                    if row.q:
                        then_next(dve.tensor_tensor(part[:, h, :], n_acc[h][0:D, :], part[:, h, :], ALU.add))
                        dve.tensor_tensor(part[:, h, :], work[0:D, h, :], part[:, h, :], ALU.add).then_inc(held_summed, 1)
                    else:
                        dve.tensor_tensor(part[:, h, :], n_acc[h][0:D, :], work[0:D, h, :], ALU.add).then_inc(held_summed, 1)

            def sum_open(row):
                if row.index:
                    dve.wait_ge(gates_ready, 2 * row.index)
                for h in range(2):
                    dve.wait_ge(low_part, 2 * row.summed_before + h + 1)
                    dve.tensor_tensor(gate_in[0:D, h, :], open_banks(row)[h][0:D, :], work[0:D, h, :],
                                      ALU.add).then_inc(open_summed, 1)

            def sum_rest(row):
                if row.index == 0:
                    return
                if row.layer == 0:
                    dve.wait_ge(adj_used, KT * row.end)
                else:
                    dve.wait_ge(part_loaded, 16 * (row.seq + 1))
                if not row.open_end:
                    dve.wait_ge(gates_ready, 2 * row.index)
                for h in range(2):
                    m = gate_in[0:D, h, :]
                    rest = part[:, h, :] if row.layer else shared_acc[h][0:D, :]
                    if row.open_end:
                        dve.wait_ge(open_summed, 2 * row.summed_before + h + 1)
                        dve.tensor_tensor(m, rest, m, ALU.add).then_inc(rest_summed, 1)
                    else:
                        dve.tensor_copy(m, rest).then_inc(rest_summed, 1)

            def pre_tanh(row):
                for h in range(2):
                    dve.wait_ge(rz_ready, 2 * row.index + h + 1)
                    then_next(dve.scalar_tensor_tensor(out=work[D:P, h, :], in0=n_acc[h][0:D, :],
                                                       scalar=bias[0:D, row.layer, 2:3], in1=rz[0:D, h, :],
                                                       op0=ALU.add, op1=ALU.mult))
                    dve.tensor_tensor(work[D:P, h, :], n_acc[h][D:P, :], work[D:P, h, :], ALU.add).then_inc(pre_ready, 1)

            def add_x(row):
                dve.wait_ge(h_turned, row.seq + 1)
                dve.wait_ge(x_row_loaded[row.seq % 2], 16 * (row.seq // 2 + 1))
                if row.seq:
                    dve.wait_ge(stored, 16 * row.seq)
                dve.tensor_tensor(summed[:, :, :], small_acc[:, :].rearrange("p (t d) -> p t d", d=D),
                                  x_row[:, row.seq % 2, :].rearrange("p (t d) -> p t d", d=D), ALU.add).then_inc(h_taken, 1)
                dve.wait_ge(h_taken, row.seq + 1)
                dve.tensor_reduce(stats[:, 0, :], summed[:, :, :], AX.X, ALU.add).then_inc(mean_ready, 1)

            def variance(row):
                if row is rows[-1]:
                    dve.wait_ge(mean_ready, NB)
                    then_next(dve.tensor_scalar(stats[:, 1, :], stats[:, 0, :], 1.0 / D, None, ALU.mult))
                    then_next(dve.tensor_tensor(summed[:, :, :], summed[:, :, :], spread(stats[:, 1, :]), ALU.subtract))
                    then_next(dve.tensor_tensor(squared[:, :, :], summed[:, :, :], summed[:, :, :], ALU.mult))
                else:
                    dve.wait_ge(squares_ready, row.seq + 1)
                dve.tensor_reduce(stats[:, 2, :], squared[:, :, :], AX.X, ALU.add).then_inc(var_ready, 1)

            def scale_last():
                dve.wait_ge(root_ready, NB)
                dve.tensor_tensor(summed[:, :, :], summed[:, :, :], spread(stats[:, 0, :]), ALU.mult).then_inc(norm_ready, 1)

            def mix_last(row):
                for h in range(2):
                    v = gate_in[D:P, h, :]
                    dve.wait_ge(n_ready, 2 * row.index + h + 1)
                    then_next(dve.tensor_tensor(v, v, fresh[D:P, h, :], ALU.subtract))
                    then_next(dve.tensor_tensor(v, v, rz[D:P, h, :], ALU.mult))
                    dve.tensor_tensor(v, v, fresh[D:P, h, :], ALU.add).then_inc(new_ready, 1)

            def block_lo(row, b):
                for k in range(NQ):
                    if b.kind != "S":
                        if k % 2 == 0:
                            stage_lo(row, b, k // 2)
                        for j in range(TQ * k, TQ * (k + 1)):
                            tile_lo(b, j)
                    if b.n is not None:
                        steps(NQ * b.w + k)

            def steps(quarter):
                for row, step in due(quarter):
                    if step == HELD_SUM:
                        sum_held(row)
                    if step == OPEN_SUM:
                        sum_open(row)
                    if step == SUM:
                        sum_rest(row)
                    if step == PRE_TANH:
                        pre_tanh(row)
                    if step == MIX and row is rows[-1]:
                        mix_last(row)
                    if step == NORM and row.layer == 1:
                        add_x(row)
                    if step == SCALE and row.layer == 1:
                        variance(row)
                    if step == SCALE and row is rows[-1]:
                        scale_last()

            work_through(dve, block_lo, steps)

        @block.gpsimd
        def _(pool):
            done = [0]

            def then_next(ins):
                done[0] += 1
                ins.then_inc(pool_step, 1)
                pool.wait_ge(pool_step, done[0])

            then_next(pool.memset(w_n[:, :, :], 0.0))
            for l in range(2):
                if l:
                    pool.dma_start(w_in[:, l, :], w[l]).then_inc(w_loaded, 16)
                for own, weights, other in ((slice(0, D), wih_t[l], slice(D, P)), (slice(D, P), whh_t[l], slice(0, D))):
                    pool.dma_start(w_rz[own, l, :], weights[:, 0:P]).then_inc(w_loaded, 16)
                    pool.dma_start(w_n[own, l, other], weights[:, P:3 * D]).then_inc(w_loaded, 16)
                for col, vec in ((0, bih), (1, bhh)):
                    pool.dma_start(bias[:, l, col:col + 1], vec[l][0:P].rearrange("(p a) -> p a", a=1)).then_inc(w_loaded, 16)
                pool.dma_start(bias[0:D, l, 2:3], bhh[l][P:3 * D].rearrange("(p a) -> p a", a=1)).then_inc(w_loaded, 16)
                pool.dma_start(bias[D:P, l, 2:3], bih[l][P:3 * D].rearrange("(p a) -> p a", a=1)).then_inc(w_loaded, 16)
            then_next(pool.memset(minus_half[:, :], -0.5))
            then_next(pool.memset(ident[:, :], 0.0))
            pool.affine_select(out=ident[:, :], in_=ident[:, :], compare_op=ALU.not_equal, fill=1.0, base=0,
                               pattern=[[-1, D]], channel_multiplier=1).then_inc(ident_ready, 1)
            pool.wait_ge(ident_ready, 1)
            pool.wait_ge(w_loaded, 16 * W_LOADS)
            for l in range(2):
                pool.tensor_tensor(bias[:, l, 3:4], bias[:, l, 0:1], bias[:, l, 1:2], ALU.add).then_inc(bias_ready, 1)
            pool.wait_ge(bias_ready, 2)

            def stage_plain(row, b):
                if b.kind == "S":
                    for g in range(2):
                        if b.plain_was is not None:
                            pool.wait_ge(adj_used, KT * b.plain_was + 4 * g + 4)
                        pool.wait_ge(z_ready, b.c + 1)
                        tiles = slice(4 * g, 4 * g + 4)
                        pool.tensor_copy(plain_w[:, tiles, :], chunk_w(b.c, tiles, slice(0, P))).then_inc(plain_ready, 1)
                if b.n is not None:
                    for k in range(NQ):
                        steps(NQ * b.w + k)

            def stages_done(quarter):
                count = 2 * sum(b.kind == "S" for row in rows for b in row.blocks if b.w <= quarter // NQ)
                if count:
                    pool.wait_ge(plain_ready, count)

            def load_v(row):
                if row.index == 0:
                    pool.wait_ge(y_product, NB)
                else:
                    pool.wait_ge(h_ready, 2 * row.index)
                source = x_t[:, row.q * CH:(row.q + 1) * CH]
                if row.layer:
                    pool.wait_ge(h_stored, 16 * (row.q + 1))
                    source = h_rows[row.q]
                pool.dma_start(gate_in[D:P, :, :].rearrange("p a n -> p (a n)"), source).then_inc(v_ready, 16)

            def store_h(row):
                pool.wait_ge(h_ready, 2 * row.index + 2)
                pool.dma_start(h_rows[row.q], fresh[0:D, :, :].rearrange("p a n -> p (a n)")).then_inc(h_stored, 16)

            def store_part(row):
                pool.wait_ge(held_summed, 2 * row.index + 2)
                pool.dma_start(part_rows[row.q], part[:, :, :].rearrange("p a n -> p (a n)")).then_inc(part_stored, 16)

            def load_part(row):
                if row.seq == 0:
                    pool.wait_ge(part_stored, 16 * NB)
                else:
                    pool.wait_ge(rest_summed, rest_count(row) - 1)
                pool.dma_start(part[:, :, :].rearrange("p a n -> p (a n)"), part_rows[row.q]).then_inc(part_loaded, 16)

            def mix(row):
                for h in range(2):
                    v = gate_in[D:P, h, :]
                    pool.wait_ge(n_ready, 2 * row.index + h + 1)
                    then_next(pool.tensor_tensor(v, v, fresh[D:P, h, :], ALU.subtract))
                    then_next(pool.tensor_tensor(v, v, rz[D:P, h, :], ALU.mult))
                    pool.tensor_tensor(v, v, fresh[D:P, h, :], ALU.add).then_inc(new_ready, 1)
                pool.wait_ge(new_ready, 2 * row.index + 2)

            def load_x(row):
                if row.seq >= 2:
                    pool.wait_ge(h_taken, row.seq - 1)
                pool.dma_start(x_row[:, row.seq % 2, :], x[row.q]).then_inc(x_row_loaded[row.seq % 2], 16)

            def center(row):
                pool.wait_ge(mean_ready, row.seq + 1)
                then_next(pool.tensor_scalar(stats[:, 1, :], stats[:, 0, :], 1.0 / D, None, ALU.mult))
                then_next(pool.tensor_tensor(summed[:, :, :], summed[:, :, :], spread(stats[:, 1, :]), ALU.subtract))
                pool.tensor_tensor(squared[:, :, :], summed[:, :, :], summed[:, :, :], ALU.mult).then_inc(squares_ready, 1)

            def scale(row):
                pool.wait_ge(var_ready, row.seq + 1)
                then_next(pool.tensor_scalar(stats[:, 3, :], stats[:, 2, :], 1.0 / D, EPS, ALU.mult, ALU.add))
                pool.tensor_tensor(stats[:, 0, :], stats[:, 3, :], minus_half[:, :], ALU.pow).then_inc(root_ready, 1)
                pool.wait_ge(root_ready, row.seq + 1)
                if row is not rows[-1]:
                    pool.tensor_tensor(summed[:, :, :], summed[:, :, :], spread(stats[:, 0, :]), ALU.mult).then_inc(norm_ready, 1)
                if row is rows[-1]:
                    return
                pool.wait_ge(norm_ready, row.seq + 1)
                pool.dma_start(out[row.q], summed[:, :, :].rearrange("p t d -> p (t d)")).then_inc(stored, 16)

            def steps(quarter):
                for row, step in due(quarter):
                    if step in (MIX, NORM):
                        stages_done(quarter)
                    if step == HELD_SUM:
                        store_part(row)
                        if row.index == NB - 1:
                            load_part(rows[NB])
                    if step == SUM and row.index == 0:
                        load_v(row)
                    if step == TURN and row is not rows[-1]:
                        load_v(rows[row.index + 1])
                        if row.index >= NB - 1:
                            load_x(rows[row.index + 1])
                    if step == SIGMOID and row.layer and row is not rows[-1]:
                        load_part(rows[row.index + 1])
                    if step == KEEP and row.layer == 0:
                        store_h(row)
                    if step == MIX and row is not rows[-1]:
                        mix(row)
                    if step == NORM and row.layer == 1 and row is not rows[-1]:
                        center(row)
                    if step == SCALE and row.layer == 1:
                        scale(row)

            work_through(pool, stage_plain, steps)

        @block.tensor
        def _(pe):
            def times_w(acc, source, l):
                for t in range(KT):
                    last = pe.matmul(acc[:, t * D:(t + 1) * D], source(t), w_in[:, l, :], start=True, stop=True)
                return last

            def make_y(group):
                for i in group:
                    if i >= len(Y_ACC):
                        pe.wait_ge(y_ready, i - len(Y_ACC) + 1)
                    times_w(y_acc(i), lambda t: x_chunk[i][:, t * P:(t + 1) * P], 0).then_inc(y_product, 1)

            pe.wait_ge(x_first, 48)
            make_y(Y_GROUPS[0])

            def split_block(row, b):
                acc = n_acc if b.kind == "H" else open_acc if b.kind == "E" else open_banks(row)
                if b.kind == "H":
                    first = last_one = True
                    pe.wait_ge(pre_ready, 2 * row.index)
                elif b.kind == "E":
                    first, last_one = b.n == row.first_early, False
                    if first:
                        pe.wait_ge(open_summed, 2 * row.summed_before)
                else:
                    first, last_one = b.n is not None and b.n == row.first_open, b.n is not None and b.n == row.last_open
                    if first and acc is n_acc:
                        pe.wait_ge(held_summed, 2 * row.index)
                    elif first and row.summed_before:
                        pe.wait_ge(open_summed, 2 * row.summed_before)
                for j in range(KT):
                    if j % 4 == 0:
                        pe.wait_ge(split_ready, 2 * b.o + j // 4 + 1)
                    pe.wait_ge(lo_ready, KT * b.o + j + 1)
                    for low in range(2):
                        for h in range(2):
                            moving = low_tile(b, j, h * HALF, HALF) if low else adj_hi[:, j, h * HALF:(h + 1) * HALF]
                            last = pe.matmul(acc[h][:, :], split_w[:, j, :], moving,
                                             start=(first and j == 0 and not low),
                                             stop=(last_one and j == KT - 1 and bool(low)))
                    last.then_inc(adj_used, 1)
                    if b.n is not None and j % TQ == TQ - 1:
                        steps(NQ * b.w + j // TQ)

            def shared_block(row, b):
                first, last_one = b.n is not None and b.n == row.first_shared, b.n is not None and b.n == row.last_shared
                if first and row.q > 1:
                    pe.wait_ge(rest_summed, rest_count(row) - 1)
                    pe.wait_ge(partial_saved, 2 * (row.q - 1))
                for j in range(KT):
                    if j % 4 == 0:
                        pe.wait_ge(plain_ready, 2 * b.s + j // 4 + 1)
                    if j % TQ == 0:
                        pe.wait_ge(adj_loaded[j // TQ], 16 * (b.l + 1))
                    for h in range(2):
                        last = pe.matmul(shared_acc[h][:, :], plain_w[:, j, :], in_tile(b, j, h * HALF, HALF),
                                         start=(first and j == 0), stop=(last_one and j == KT - 1))
                    last.then_inc(adj_used, 1)
                    if b.n is not None and j % TQ == TQ - 1:
                        steps(NQ * b.w + j // TQ)

            def multiply(row, b):
                if b.kind == "S":
                    shared_block(row, b)
                else:
                    split_block(row, b)

            def gates(row):
                if row.index == 0:
                    pe.wait_ge(w_loaded, 16 * W_LOADS)
                pe.wait_ge(v_ready, 16 * (row.index + 1))
                if row.index:
                    pe.wait_ge(held_summed, 2 * min(row.index, NB))
                for h in range(2):
                    if row.open_end:
                        pe.wait_ge(open_summed, 2 * row.summed_before + h + 1)
                    if row.index:
                        pe.wait_ge(rest_summed, rest_count(row) + h)
                    if h == 0 and 0 < row.index <= NB:
                        pe.wait_ge(z_ready, row.index)
                    if h == 0 and row.index > NB:
                        pe.wait_ge(h_taken, row.seq)
                    pe.matmul(rz_acc[h][:, :], w_rz[:, row.layer, :], gate_in[:, h, :], start=True, stop=True)
                    pe.matmul(n_acc[h][:, :], w_n[:, row.layer, :], gate_in[:, h, :],
                              start=True, stop=True).then_inc(gates_ready, 1)

            def make_z(row):
                pe.wait_ge(h_ready, 2 * row.index + 2)
                both = fresh[0:D, :, :].rearrange("d h n -> d (h n)")
                times_w(small_acc, lambda t: both[:, t * P:(t + 1) * P], 1).then_inc(z_product, 1)

            def turn(row):
                if row.seq == 0:
                    pe.wait_ge(ident_ready, 1)
                pe.wait_ge(h_ready, 2 * row.index + 2)
                both = fresh[0:D, :, :].rearrange("d h n -> d (h n)").rearrange("d (p i) -> d i p", i=KT)
                for i in range(KT):
                    last = pe.transpose(small_acc[:, i * D:(i + 1) * D], both[:, i, :], ident[:, :])
                last.then_inc(h_turned, 1)

            def steps(quarter):
                if quarter in Y_MADE:
                    if quarter == Y_MADE[0]:
                        pe.wait_ge(x_rest, 16 * (NB - len(Y_GROUPS[0])))
                    make_y(Y_GROUPS[Y_MADE.index(quarter) + 1])
                for row, step in due(quarter):
                    if step == GATES:
                        gates(row)
                    if step == TURN and row.layer == 0:
                        make_z(row)
                    if step == TURN and row.layer == 1:
                        turn(row)

            work_through(pe, multiply, steps)


def kernel(**inputs):
    import numpy as np
    import concourse.bacc as bacc
    from concourse.bass_utils import run_bass_kernel_spmd as run

    def get(name):
        return np.asarray(inputs[name])

    adj = get("adj").reshape(NB, CH, NB, NQ, TQ, P).transpose(0, 2, 3, 5, 4, 1).reshape(NB, NB, NQ, P, TQ * CH)
    arrays = {"adj_t": np.ascontiguousarray(adj),
              "x_t": np.ascontiguousarray(get("x").T),
              "x": get("x").reshape(NB, P, KT * D)}
    for l in (1, 2):
        arrays[f"w{l}"] = get(f"L0_gnn_W{l}")
        arrays[f"wih_t{l}"] = np.ascontiguousarray(get(f"L0_gnn_wih{l}").T)
        arrays[f"whh_t{l}"] = np.ascontiguousarray(get(f"L0_gnn_whh{l}").T)
        arrays[f"bih{l}"] = get(f"L0_gnn_bih{l}")
        arrays[f"bhh{l}"] = get(f"L0_gnn_bhh{l}")

    nc = bacc.Bacc("TRN2", target_bir_lowering=False, num_devices=1)
    ap = {name: nc.dram_tensor(name, a.shape, mybir.dt.from_np(a.dtype), kind="ExternalInput").ap()
          for name, a in arrays.items()}
    out = nc.dram_tensor("out", (NB, P, KT * D), F32, kind="ExternalOutput").ap()
    h_rows = nc.dram_tensor("h_rows", (NB, D, CH), F32).ap()
    part_rows = nc.dram_tensor("part_rows", (NB, D, CH), F32).ap()
    gated_graph_layers(nc, ap["adj_t"], ap["x_t"], ap["x"], [ap["w1"], ap["w2"]],
                       [ap["wih_t1"], ap["wih_t2"]], [ap["whh_t1"], ap["whh_t2"]],
                       [ap["bih1"], ap["bih2"]], [ap["bhh1"], ap["bhh2"]], h_rows, part_rows, out)
    r = run(nc, [arrays], core_ids=[0])
    return r.results[0]["out"].reshape(N, D)
```
